# Optimizing a Trainium2 kernel written in Bass

```python
import numpy as np
import jax
import jax.numpy as jnp

def _softmax(x, axis=-1):
    return jax.nn.softmax(x, axis=axis)

def _gelu(x):
    return jax.nn.gelu(x, approximate=True)

def _silu(x):
    return jax.nn.silu(x)

def _sigmoid(x):
    return jax.nn.sigmoid(x)

def _layernorm(x, axis=-1, eps=1e-05):
    m = jnp.mean(x, axis=axis, keepdims=True)
    v = jnp.var(x, axis=axis, keepdims=True)
    return (x - m) / jnp.sqrt(v + eps)

def _scatter_add(tgt, idx, src, axis=0):
    return tgt.at[idx].add(src)

def _segment_sum(src, seg, n):
    return jax.ops.segment_sum(src, seg, n)
kernel_name = 'mk_adaln_d1_jaxref_r8_02c83b'

def setup_inputs(seed: int=0):
    np.random.seed(seed)
    _w = jnp.asarray

    def _L0_attn_setup():
        import jax, jax.numpy as jnp
        import numpy as np
        H, KV, HD, HID = (32, 8, 128, 512)
        THETA, FACTOR, HI_FF, LO_FF, ORIG_MAX = (500000.0, 8.0, 4.0, 1.0, 1024)

        def _llama3_inv_freq():
            inv = 1.0 / THETA ** (np.arange(0, HD, 2, dtype=np.float64) / HD)
            wavelen = 2.0 * np.pi / inv
            low_wl = ORIG_MAX / LO_FF
            high_wl = ORIG_MAX / HI_FF
            smooth = (ORIG_MAX / wavelen - LO_FF) / (HI_FF - LO_FF)
            scaled = np.where(wavelen > low_wl, inv / FACTOR, inv)
            mid = (wavelen <= low_wl) & (wavelen >= high_wl)
            scaled = np.where(mid, (1 - smooth) * inv / FACTOR + smooth * inv, scaled)
            return scaled.astype(np.float32)

        def _rope_cos_sin(T):
            inv = _llama3_inv_freq()
            pos = np.arange(T, dtype=np.float32)
            freqs = pos[:, None] * inv[None, :]
            emb = np.concatenate([freqs, freqs], axis=-1)
            return (jnp.asarray(np.cos(emb)), jnp.asarray(np.sin(emb)))

        def _rotate_half(x):
            x1, x2 = jnp.split(x, 2, axis=-1)
            return jnp.concatenate([-x2, x1], axis=-1)
        key = jax.random.key(seed)
        ks = jax.random.split(key, 5)
        s = 1.0 / np.sqrt(HID)
        return {'x': jax.random.normal(ks[0], (1, 256, HID), jnp.float32), 'wq': jax.random.normal(ks[1], (HID, H * HD), jnp.float32) * s, 'wk': jax.random.normal(ks[2], (HID, KV * HD), jnp.float32) * s, 'wv': jax.random.normal(ks[3], (HID, KV * HD), jnp.float32) * s, 'wo': jax.random.normal(ks[4], (H * HD, HID), jnp.float32) * s}
    _L0_attn_in = _L0_attn_setup()

    def _L0_ffn_setup():
        import jax, jax.numpy as jnp
        import numpy as np
        M = 512
        K = 512

        def _make_2to4_mask(key, shape):
            scores = jax.random.normal(key, shape)
            g = scores.reshape(shape[0], shape[1] // 4, 4)
            rank = jnp.argsort(jnp.argsort(-jnp.abs(g), axis=-1), axis=-1)
            return (rank < 2).reshape(shape).astype(jnp.float32)
        key = jax.random.key(seed)
        k_x, k_w12, k_b12, k_w3, k_b3, k_m = jax.random.split(key, 6)
        x = jax.random.normal(k_x, (4, 256, K), dtype=jnp.float32)
        w12_dense = jax.random.normal(k_w12, (2 * M, K), dtype=jnp.float32) * (1.0 / np.sqrt(K))
        mask12 = _make_2to4_mask(k_m, (2 * M, K))
        w12 = w12_dense * mask12
        b12 = jax.random.normal(k_b12, (2 * M,), dtype=jnp.float32) * 0.01
        w3 = jax.random.normal(k_w3, (M, M), dtype=jnp.float32) * (1.0 / np.sqrt(M))
        b3 = jax.random.normal(k_b3, (M,), dtype=jnp.float32) * 0.01
        return {'x': x, 'w12': w12, 'b12': b12, 'w3': w3, 'b3': b3}
    _L0_ffn_in = _L0_ffn_setup()
    _L0_c = _w((lambda *s: np.random.randn(*s).astype(np.float32) * 0.05)(2, 512))
    _L0_wmod = _w((lambda *s: np.random.randn(*s).astype(np.float32) * 0.05)(512, 6 * 512) * 512 ** (-0.5))
    _d = {'L0_attn_x': _L0_attn_in['x'], 'L0_attn_wq': _L0_attn_in['wq'], 'L0_attn_wk': _L0_attn_in['wk'], 'L0_attn_wv': _L0_attn_in['wv'], 'L0_attn_wo': _L0_attn_in['wo'], 'L0_ffn_w12': _L0_ffn_in['w12'], 'L0_ffn_b12': _L0_ffn_in['b12'], 'L0_ffn_w3': _L0_ffn_in['w3'], 'L0_ffn_b3': _L0_ffn_in['b3'], 'L0_c': _L0_c, 'L0_wmod': _L0_wmod}
    _x0 = _d['L0_attn_x']
    _d['L0_attn_x'] = jax.random.normal(jax.random.fold_in(jax.random.key(seed), 1), (2, 512, 512), dtype=_x0.dtype)
    del _x0
    return _d

def reference(L0_attn_x, L0_attn_wq, L0_attn_wk, L0_attn_wv, L0_attn_wo, L0_ffn_w12, L0_ffn_b12, L0_ffn_w3, L0_ffn_b3, L0_c, L0_wmod):

    def _L0_attn_ref(x, wq, wk, wv, wo):
        import jax, jax.numpy as jnp
        import numpy as np
        H, KV, HD, HID = (32, 8, 128, 512)
        THETA, FACTOR, HI_FF, LO_FF, ORIG_MAX = (500000.0, 8.0, 4.0, 1.0, 1024)

        def _llama3_inv_freq():
            inv = 1.0 / THETA ** (np.arange(0, HD, 2, dtype=np.float64) / HD)
            wavelen = 2.0 * np.pi / inv
            low_wl = ORIG_MAX / LO_FF
            high_wl = ORIG_MAX / HI_FF
            smooth = (ORIG_MAX / wavelen - LO_FF) / (HI_FF - LO_FF)
            scaled = np.where(wavelen > low_wl, inv / FACTOR, inv)
            mid = (wavelen <= low_wl) & (wavelen >= high_wl)
            scaled = np.where(mid, (1 - smooth) * inv / FACTOR + smooth * inv, scaled)
            return scaled.astype(np.float32)

        def _rope_cos_sin(T):
            inv = _llama3_inv_freq()
            pos = np.arange(T, dtype=np.float32)
            freqs = pos[:, None] * inv[None, :]
            emb = np.concatenate([freqs, freqs], axis=-1)
            return (jnp.asarray(np.cos(emb)), jnp.asarray(np.sin(emb)))

        def _rotate_half(x):
            x1, x2 = jnp.split(x, 2, axis=-1)
            return jnp.concatenate([-x2, x1], axis=-1)
        B, T, _ = x.shape
        q = (x @ wq).reshape(B, T, H, HD).transpose(0, 2, 1, 3)
        k = (x @ wk).reshape(B, T, KV, HD).transpose(0, 2, 1, 3)
        v = (x @ wv).reshape(B, T, KV, HD).transpose(0, 2, 1, 3)
        cos, sin = _rope_cos_sin(T)
        q = q * cos + _rotate_half(q) * sin
        k = k * cos + _rotate_half(k) * sin
        rep = H // KV
        k = jnp.repeat(k, rep, axis=1)
        v = jnp.repeat(v, rep, axis=1)
        scores = jnp.einsum('bhtd,bhsd->bhts', q, k) * (1.0 / np.sqrt(HD))
        mask = jnp.tril(jnp.ones((T, T), dtype=bool))
        scores = jnp.where(mask, scores, -jnp.inf)
        att = jax.nn.softmax(scores, axis=-1)
        out = jnp.einsum('bhts,bhsd->bhtd', att, v)
        out = out.transpose(0, 2, 1, 3).reshape(B, T, H * HD)
        return out @ wo

    def _L0_ffn_ref(x, w12, b12, w3, b3):
        import jax, jax.numpy as jnp
        import numpy as np
        M = 512
        K = 512

        def _make_2to4_mask(key, shape):
            scores = jax.random.normal(key, shape)
            g = scores.reshape(shape[0], shape[1] // 4, 4)
            rank = jnp.argsort(jnp.argsort(-jnp.abs(g), axis=-1), axis=-1)
            return (rank < 2).reshape(shape).astype(jnp.float32)
        x12 = jnp.einsum('bsk,mk->bsm', x, w12) + b12
        x1, x2 = jnp.split(x12, 2, axis=-1)
        x4 = jax.nn.silu(x1) * x2
        return jnp.einsum('bsm,nm->bsn', x4, w3) + b3
    x = L0_attn_x
    mod = (_silu(L0_c) @ L0_wmod).reshape(L0_c.shape[0], 6, 1, -1)
    sa, ca, ga, sb, cb, gb = (mod[:, 0], mod[:, 1], mod[:, 2], mod[:, 3], mod[:, 4], mod[:, 5])
    ga = (2 * (ga >= 0) - 1) * jnp.maximum(jnp.abs(ga), 0.25)
    gb = (2 * (gb >= 0) - 1) * jnp.maximum(jnp.abs(gb), 0.25)
    h = _layernorm(x, axis=-1) * (1 + ca) + sa
    x = x + ga * _L0_attn_ref(h, L0_attn_wq, L0_attn_wk, L0_attn_wv, L0_attn_wo)
    h = _layernorm(x, axis=-1) * (1 + cb) + sb
    x = x + gb * _L0_ffn_ref(h, L0_ffn_w12, L0_ffn_b12, L0_ffn_w3, L0_ffn_b3)
    return x

_drawn_inputs = setup_inputs


def setup_inputs(seed=0):
    import zlib

    import numpy as np

    out = dict(_drawn_inputs(seed))
    spreads = {}
    factors = {'L0_ffn_b12': 31.663, 'L0_ffn_b3': 23.355}
    for name, (base, spread) in spreads.items():
        noise = np.random.default_rng([zlib.crc32(name.encode()), seed]).standard_normal(out[name].shape)
        drawn = base * np.exp(spread * noise) if base else spread * noise
        out[name] = jnp.asarray(drawn.astype(out[name].dtype))
    for name, factor in factors.items():
        out[name] = (out[name] * factor).astype(out[name].dtype)
    return out
```

```python
import concourse.bass as bass
from concourse import mybir
from contextlib import ExitStack
import numpy as np

B, T, HID = 2, 512, 512
H, KV, HD = 32, 8, 128
FF = 512
P = 128
TT = T // P
KC = HID // P
REP = H // KV
STEPS = B * REP
EPS = 1e-5
SCALE = 1.0 / float(np.sqrt(HD))
MASKED = -1.0e30
LOWEST = -3.0e38

ROW_W = [P * (i + 1) for i in range(TT)]
ROW_AT = [sum(ROW_W[:i]) for i in range(TT)]
ROWS = sum(ROW_W)
COL_W = [T - P * j for j in range(TT)]
COL_AT = {0: 0, 1: COL_W[0], 3: COL_W[0] + COL_W[1], 2: COL_W[0] + COL_W[1] + COL_W[3]}
T_BANKS = [(0, T), (T, 2 * T), (2 * T, ROWS)]


def adaln_block(nc, x, wq, wk, wv, wo, w12, b12, w3, b3, c, wmod, cos_t, sin_t, mask_t, ident_t, out):
    f32, f32r, i32 = mybir.dt.float32, mybir.dt.float32r, mybir.dt.int32
    ALU, ACT = mybir.AluOpType, mybir.ActivationFunctionType

    x_tiles = x.rearrange("b (i p) f -> p (b i) f", p=P)
    out_tiles = out.rearrange("b (i p) f -> p (b i) f", p=P)
    wq_v = wq.rearrange("(k p) n -> p k n", p=P)
    wk_v = wk.rearrange("(k p) n -> p k n", p=P)
    wv_v = wv.rearrange("(k p) n -> p k n", p=P)
    wo_v = wo.rearrange("(h p) n -> p h n", p=P)
    wmod_v = wmod.rearrange("(k p) n -> p k n", p=P)
    w12_v = w12.rearrange("(m p) k -> p m k", p=P)
    w3_v = w3.rearrange("(n p) m -> p n m", p=P)

    st = ExitStack()
    with st:
        def sb(name, shape, dt=f32):
            return st.enter_context(nc.sbuf_tensor(name, shape, dt))

        def sem(name):
            return st.enter_context(nc.semaphore(name))

        cos_sb = sb("cos_sb", [P, T])
        sin_sb = sb("sin_sb", [P, T])
        mask_sb = sb("mask_sb", [P, T])
        ident = sb("ident", [P, P])
        acc = sb("acc", [P, B * TT, HID])
        wq_raw = sb("wq_raw", [P, KC, REP * HD])
        wk_raw = sb("wk_raw", [P, KC, HD])
        wv_raw = sb("wv_raw", [P, KC, HD])
        wo_raw = sb("wo_raw", [P, REP, HID])
        hT = [sb(f"hT_{s}", [P, KC, B * T], f32r) for s in ("hi", "lo")]
        wq_s = [sb(f"wq_{s}", [P, REP, KC, HD], f32r) for s in ("hi", "lo")]
        wk_s = [sb(f"wk_{s}", [P, KC, HD], f32r) for s in ("hi", "lo")]
        wv_s = [sb(f"wv_{s}", [P, KC, HD], f32r) for s in ("hi", "lo")]
        with nc.sbuf_tensor("wmod_a", [P, KC, 2 * HID], f32) as wmod_a:
            pass
        wo_s = [sb(f"wo_{s}", [P, REP, HID], f32r) for s in ("hi", "lo")]
        wmod_b = acc[:, :, :].rearrange("p (k a) n -> p k (a n)", k=KC)
        kT = [sb(f"kT_{s}", [P, B, T], f32r) for s in ("hi", "lo")]
        v_s = [sb(f"v_{s}", [P, B, TT, HD], f32r) for s in ("hi", "lo")]
        qT = [sb(f"qT_{s}", [P, 2, T], f32r) for s in ("hi", "lo")]
        attn = [sb(f"attn_{s}", [P, STEPS, T], f32r) for s in ("hi", "lo")]
        pT = [sb(f"pT_{s}", [P, ROWS], f32r) for s in ("hi", "lo")]
        probs = sb("probs", [P, 2, ROWS])
        q_tmp = sb("q_tmp", [P, 2, 2, T])
        k_tmp = sb("k_tmp", [P, 2, T])
        vT = sb("vT", [P, T])
        cT = sb("cT", [P, KC, B])
        c_exp = sb("c_exp", [P, KC, B])
        c_silu = sb("c_silu", [P, KC, B])
        mod = sb("mod", [P, 6 * KC, B])
        one_plus = sb("one_plus", [P, 2 * KC, B])
        gate_sign = sb("gate_sign", [P, 2 * KC, B])
        gate = sb("gate", [P, 2 * KC, B])
        b12T = sb("b12T", [P, 2 * FF // P])
        neg_b1 = sb("neg_b1", [P, FF // P])
        stats = sb("stats", [P, B * TT, 6])
        moments = sb("moments", [P, B * TT, 2])
        rstd = sb("rstd", [P, B * TT, 1])
        var_eps = sb("var_eps", [P, B * TT, 1])
        newton = sb("newton", [P, B * TT, 1])
        wait_mark = sb("wait_mark", [P, 2, 3])
        row_max = sb("row_max", [P, 2, TT])
        neg_max = sb("neg_max", [P, 2, TT])
        row_sum = sb("row_sum", [P, 2, TT])
        row_inv = sb("row_inv", [P, 2, TT])

        def bank(name):
            return st.enter_context(nc.psum_tensor(name, [P, 512], f32))

        s_row1, s_row20, s_row3 = bank("s_row1"), bank("s_row20"), bank("s_row3")
        t_col0, t_col13 = bank("t_col0"), bank("t_col13")
        q_bank, x_bank, o_bank = bank("q_bank"), bank("x_bank"), bank("o_bank")
        s_out = [s_row20[:, ROW_W[2]:T], s_row1[:, 0:ROW_W[1]], s_row20[:, 0:ROW_W[2]], s_row3[:, :]]
        t_out = {0: t_col0[:, :], 1: t_col13[:, 0:COL_W[1]], 3: t_col13[:, COL_W[1]:T],
                 2: s_row1[:, T - COL_W[2]:T]}
        t_banks = [t_col0[:, :], t_col13[:, :], s_row1[:, T - COL_W[2]:T]]
        ln_banks = [[s_row1, s_row20, s_row3, t_col0], [t_col13, q_bank, o_bank, s_row1]]

        tables_in, x_in, c_in, wmod_in, wmod_b_in, b_in = (
            sem("tables_in"), [sem(f"x_in{b}") for b in range(B)], sem("c_in"), sem("wmod_in"),
            sem("wmod_b_in"), sem("b_in"))
        wq_in, wk_in, wv_in, wo_in = sem("wq_in"), sem("wk_in"), sem("wv_in"), sem("wo_in")
        wq_hi, wq_lo, wk_hi, wk_lo = sem("wq_hi"), sem("wq_lo"), sem("wk_hi"), sem("wk_lo")
        wv_hi, wv_lo, wo_hi, wo_lo = sem("wv_hi"), sem("wv_lo"), sem("wo_hi"), sem("wo_lo")
        dve_chain = sem("dve_chain")
        c_exped, c_ready, mod_made, mod_read, mod_ready = (
            sem("c_exped"), sem("c_ready"), sem("mod_made"), sem("mod_read"), sem("mod_ready"))
        moments_ready = sem("moments_ready")
        x_normed, x_turned, h_ready, h_hi, h_lo = (
            sem("x_normed"), sem("x_turned"), sem("h_ready"), sem("h_hi"), sem("h_lo"))
        k_proj, k_rot, k_sum, k_hi, k_lo = sem("k_proj"), sem("k_rot"), sem("k_sum"), sem("k_hi"), sem("k_lo")
        v_proj, v_copied, v_turned, v_hi, v_lo = (
            sem("v_proj"), sem("v_copied"), sem("v_turned"), sem("v_hi"), sem("v_lo"))
        q_proj, q_rot, q_sum, q_hi, q_lo = sem("q_proj"), sem("q_rot"), sem("q_sum"), sem("q_hi"), sem("q_lo")
        scores_ready, rows_maxed, negmax_ready, exp_done = (
            sem("scores_ready"), sem("rows_maxed"), sem("negmax_ready"), sem("exp_done"))
        inv_ready, probs_normed = sem("inv_ready"), sem("probs_normed")
        pT_turned, pT_hi, pT_lo = sem("pT_turned"), sem("pT_hi"), sem("pT_lo")
        attn_done, attn_hi, attn_lo = sem("attn_done"), sem("attn_hi"), sem("attn_lo")
        wo_made, wo_added = sem("wo_made"), sem("wo_added")
        w12_in, w3_in, f_turned, f_hi, f_lo = sem("w12_in"), sem("w3_in"), sem("f_turned"), sem("f_hi"), sem("f_lo")
        gate_wide, gate_turned, gate_copied = sem("gate_wide"), sem("gate_turned"), sem("gate_copied")
        xr_in = [sem(f"xr_in{i}") for i in range(2)]
        x_used, x1_normed, h2_turned, h2_ready, h2_hi, h2_lo = (
            sem("x_used"), sem("x1_normed"), sem("h2_turned"), sem("h2_ready"), sem("h2_hi"), sem("h2_lo"))
        b3_in, up_made, e_made, u_made, x4_made, x4_hi, x4_lo = (
            sem("b3_in"), sem("up_made"), sem("e_made"), sem("u_made"), sem("x4_made"), sem("x4_hi"), sem("x4_lo"))
        down_made, y_made, y_stored = sem("down_made"), sem("y_made"), sem("y_stored")

        w12T = hT
        w3T = [w[:, :, :, :].rearrange("p r k d -> p r (k d)") for w in wq_s]
        h2T = attn
        k_flat = [k[:, :, :] for k in kT]
        v_flat = [v[:, :, :, :].rearrange("p b i d -> p b (i d)") for v in v_s]

        def x4_at(part, b, mc):
            if b == 1:
                return wo_s[part][:, mc, :]
            return (k_flat, v_flat)[mc // 2][part][:, mc % 2, :]

        xn2 = q_tmp[:, :, :, :].rearrange("p s c t -> p (s c) t")
        h2_tmp = k_tmp
        x_ring = [wk_raw[:, :, :].rearrange("p k d -> p (k d)"), wv_raw[:, :, :].rearrange("p k d -> p (k d)")]
        p_flat = probs[:, :, :].rearrange("p s n -> p (s n)")
        gate_w = [[p_flat[:, (2 * a + b) * HID:(2 * a + b + 1) * HID] for b in range(B)] for a in range(2)]
        b3_w = p_flat[:, 4 * HID:5 * HID]

        PARTS = [(0, 0), (0, 1), (1, 0)]

        def need(eng, s, per, g, off):
            if isinstance(g, int):
                if per * g + off > 0:
                    eng.wait_ge(s, per * g + off)
            elif per + off > 0:
                eng.wait_ge(s, g * per + off)
            else:
                assert per * (KV - 2) + off <= 0

        def head(j):
            return j // STEPS, j % STEPS // REP, j % REP

        h2_banks = [t_col13, q_bank, x_bank, o_bank]
        up_banks = [s_row1, s_row20, s_row3, t_col0]
        up_raw = [wq_raw[:, :, :], wo_raw[:, :, :]]
        up_tmp = [(up_raw[s][:, 0, :], up_raw[s][:, 1, :]) for s in range(2)]

        def f_place(u):
            if u < 2 * KC:
                at = (u // KC) * FF
                return [w12T[s][:, u % KC, at:at + FF] for s in range(2)]
            return [w3T[s][:, u - 2 * KC, :] for s in range(2)]

        block = st.enter_context(nc.Block())

        @block.sync
        def _(sp):
            for b in range(B):
                sp.dma_start(acc[:, TT * b:TT * (b + 1), :], x_tiles[:, TT * b:TT * (b + 1), :]).then_inc(x_in[b], 16)
                if b == 0:
                    sp.dma_start(wmod_a[:, :, :], wmod_v[:, :, 0:2 * HID]).then_inc(wmod_in, 16)
            sp.dma_start(wk_raw[:, :, :], wk_v[:, :, 0:HD]).then_inc(wk_in, 16)
            sp.dma_start(wq_raw[:, :, :], wq_v[:, :, 0:REP * HD]).then_inc(wq_in, 16)
            sp.dma_start(wv_raw[:, :, :], wv_v[:, :, 0:HD]).then_inc(wv_in, 16)
            sp.wait_ge(x_turned, B * KC)
            sp.dma_start(wmod_b, wmod_v[:, :, 2 * HID:4 * HID]).then_inc(wmod_b_in, 16)
            sp.wait_ge(mod_made, 2)
            sp.dma_start(wmod_a[:, :, :], wmod_v[:, :, 4 * HID:6 * HID]).then_inc(wmod_in, 16)
            sp.dma_start(wo_raw[:, :, :], wo_v[:, 0:REP, :]).then_inc(wo_in, 16)

            def next_weights(g):
                need(sp, wk_lo, 1, g, 1)
                sp.dma_start(wk_raw[:, :, :], wk_v[:, :, bass.ds((g + 1) * HD, HD)]).then_inc(wk_in, 16)
                need(sp, wq_lo, REP, g, REP)
                sp.dma_start(wq_raw[:, :, :], wq_v[:, :, bass.ds((g + 1) * (REP * HD), REP * HD)]).then_inc(wq_in, 16)
                need(sp, wv_lo, 1, g, 1)
                sp.dma_start(wv_raw[:, :, :], wv_v[:, :, bass.ds((g + 1) * HD, HD)]).then_inc(wv_in, 16)
                need(sp, wo_lo, REP, g, REP)
                sp.dma_start(wo_raw[:, :, :], wo_v[:, bass.ds((g + 1) * REP, REP), :]).then_inc(wo_in, 16)

            next_weights(0)
            with sp.Fori(1, KV - 1) as g:
                next_weights(g)
            sp.wait_ge(wq_lo, REP * KV)
            sp.dma_start(wq_raw[:, :, :], w12_v[:, 0:4, :]).then_inc(w12_in, 16)
            sp.wait_ge(wo_lo, REP * KV)
            sp.dma_start(wo_raw[:, :, :], w12_v[:, 4:8, :]).then_inc(w12_in, 16)
            for w in range(B * TT):
                if w == 0:
                    sp.wait_ge(wk_lo, KV)
                if w == 1:
                    sp.wait_ge(wv_lo, KV)
                if w >= 2:
                    sp.wait_ge(x_used, w - 1)
                sp.dma_start(x_ring[w % 2], x_tiles[:, w, :]).then_inc(xr_in[w % 2], 16)
                if w == 1:
                    sp.wait_ge(f_turned, KC)
                    sp.dma_start(wq_raw[:, :, :], w3_v).then_inc(w3_in, 16)
            for w in range(B * TT):
                sp.wait_ge(y_made, w + 1)
                sp.dma_start(out_tiles[:, w, :], acc[:, w, :]).then_inc(y_stored, 16)
            sp.wait_ge(y_stored, 16 * B * TT)

        @block.tensor
        def _(pe):
            def product(dst, lhs, rhs, chunks):
                todo = [(cc, a, b) for cc in chunks for a, b in PARTS]
                for k, (cc, a, b) in enumerate(todo):
                    last = pe.matmul(dst, lhs(a, cc), rhs(b, cc), start=(k == 0), stop=(k == len(todo) - 1))
                return last

            def modulation(slab, first, count, dst):
                for m in range(count):
                    for k in range(KC):
                        last = pe.matmul(dst[:, 2 * (first + m):2 * (first + m) + 2], slab[:, k, m * P:(m + 1) * P],
                                         c_silu[:, k, :], start=(k == 0), stop=(k == KC - 1))
                last.then_inc(mod_made, 1)

            def project_k(g, b, m_off):
                need(pe, wk_lo, 1, g, m_off // 2 + 1)
                product(x_bank[:, :], lambda a, k: wk_s[a][:, k, :],
                        lambda a, k: hT[a][:, k, b * T:(b + 1) * T], range(KC)).then_inc(k_proj, 1)

            def project_v(g, b, m_off):
                need(pe, wv_lo, 1, g, m_off // 2 + 1)
                product(x_bank[:, :], lambda a, k: wv_s[a][:, k, :],
                        lambda a, k: hT[a][:, k, b * T:(b + 1) * T], range(KC)).then_inc(v_proj, 1)

            def turn_v(g, m_off):
                need(pe, v_copied, 2, g, m_off + 1)
                for i in range(TT):
                    last = pe.transpose(x_bank[:, i * P:(i + 1) * P], vT[:, i * P:(i + 1) * P], ident[:, :])
                last.then_inc(v_turned, 1)

            def project_q(g, j):
                ahead, b, h = head(j)
                need(pe, q_rot, STEPS, g, j)
                need(pe, wq_lo, REP, g, REP * ahead + h + 1)
                product(q_bank[:, :], lambda a, k: wq_s[a][:, h, k, :],
                        lambda a, k: hT[a][:, k, b * T:(b + 1) * T], range(KC)).then_inc(q_proj, 1)

            def scores(g, j):
                _, b, h = head(j)
                need(pe, q_lo, STEPS, g, j + 1)
                if h == 0:
                    need(pe, k_lo, 2, g, b + 1)
                need(pe, rows_maxed, 3 * STEPS, g, 3 * j)
                need(pe, pT_lo, 3 * STEPS, g, 3 * (j - 1))
                for tiles in ((1,), (2, 0), (3,)):
                    for i in tiles:
                        last = product(s_out[i], lambda a, _: qT[a][:, j % 2, i * P:(i + 1) * P],
                                       lambda a, _: kT[a][:, b, 0:ROW_W[i]], [0])
                    last.then_inc(scores_ready, 1)

            def turn_probs(g, j, final=False):
                need(pe, probs_normed, STEPS, g, j + 1)
                need(pe, pT_lo, 3 * STEPS, g, 3 * j)
                for cols in ((0,), (1, 3), (2,)):
                    if cols == (2,):
                        need(pe, rows_maxed, 3 * STEPS, g, 3 * (j + 1) + (0 if final else 1))
                    for jj in cols:
                        for i in range(jj, TT):
                            at = ROW_AT[i] + jj * P
                            last = pe.transpose(t_out[jj][:, (i - jj) * P:(i - jj + 1) * P],
                                                probs[:, j % 2, at:at + P], ident[:, :])
                    last.then_inc(pT_turned, 1)

            def attend(g, j):
                _, b, h = head(j)
                need(pe, attn_lo, STEPS, g, j)
                if h == 0:
                    need(pe, v_lo, 2, g, b + 1)
                for k, cols in enumerate(((0,), (1, 3), (2,))):
                    need(pe, pT_lo, 3 * STEPS, g, 3 * j + k + 1)
                    for jj in cols:
                        for a, bb in PARTS:
                            last = pe.matmul(o_bank[:, jj * P:T], v_s[a][:, b, jj, :],
                                             pT[bb][:, COL_AT[jj]:COL_AT[jj] + COL_W[jj]],
                                             start=(jj == 0 and (a, bb) == PARTS[0]),
                                             stop=(jj == 2 and (a, bb) == PARTS[-1]))
                last.then_inc(attn_done, 1)

            def project_out(g, b, i, dst, g_off=0):
                need(pe, attn_lo, STEPS, g, STEPS * g_off + REP * (b + 1))
                need(pe, wo_lo, REP, g, REP * (g_off + 1))
                product(dst, lambda a, h: attn[a][:, REP * b + h, i * P:(i + 1) * P],
                        lambda a, h: wo_s[a][:, h, :], range(REP)).then_inc(wo_made, 1)

            def free_x_after_wo(g, w_off):
                need(pe, wo_added, STEPS, g, w_off)

            def group(g, first=False, last=False):
                for j in range(STEPS):
                    scores(g, j)
                    if not (first and j == 0):
                        turn_probs(g, j - 1)
                    if not (last and j + 2 >= STEPS):
                        project_q(g, j + 2)
                    if j == 0:
                        if first:
                            need(pe, v_lo, 2, g, 1)
                        else:
                            need(pe, v_lo, 2, g, 1)
                        project_k(g, 1, 1)
                    if j in (1, 2) and not first:
                        if j == 1:
                            need(pe, k_rot, 2, g, 2)
                        free_x_after_wo(g, STEPS * 0 - TT + 2 * (j - 1))
                        project_out(g, 1, 2 * (j - 1), x_bank[:, :], g_off=-1)
                    if first and j == 2:
                        need(pe, k_rot, 2, g, 2)
                        pe.wait_ge(wmod_b_in, 16)
                        modulation(wmod_b, 2 * KC, 2 * KC, x_bank)
                        pe.wait_ge(wmod_in, 32)
                        modulation(wmod_a, 4 * KC, 2 * KC, x_bank)
                    if j == 3:
                        if first:
                            pe.wait_ge(mod_read, 2)
                        else:
                            free_x_after_wo(g, 0)
                        project_v(g, 1, 1)
                    if j == 4 and not last:
                        need(pe, v_lo, 2, g, 2)
                        project_k(g, 0, 2)
                    if j in (5, 6):
                        if j == 5 and not last:
                            need(pe, k_rot, 2, g, 3)
                        if j == 5 and last:
                            need(pe, v_lo, 2, g, 2)
                        free_x_after_wo(g, 2 * (j - 5))
                        project_out(g, 0, 2 * (j - 5), x_bank[:, :])
                    if j == 7 and not last:
                        free_x_after_wo(g, TT)
                        project_v(g, 0, 2)
                    if not (first and j == 0):
                        attend(g, j - 1)
                    if j in (1, 2) and not first:
                        free_x_after_wo(g, -TT + 2 * (j - 1) + 1)
                        project_out(g, 1, 2 * (j - 1) + 1, x_bank[:, :], g_off=-1)
                    if j == 3:
                        turn_v(g, 1)
                    if j in (5, 6):
                        free_x_after_wo(g, 2 * (j - 5) + 1)
                        project_out(g, 0, 2 * (j - 5) + 1, x_bank[:, :])
                    if j == 7 and not last:
                        turn_v(g, 2)
                    if j == 7 and last:
                        free_x_after_wo(g, TT)
                        need(pe, q_rot, STEPS, g, STEPS)

            pe.wait_ge(tables_in, 64)
            pe.wait_ge(c_ready, 1)
            pe.wait_ge(wmod_in, 16)
            modulation(wmod_a, 0, KC, x_bank)
            modulation(wmod_a[:, :, HID:2 * HID], KC, KC, x_bank)
            for b in range(B):
                pe.wait_ge(x_normed, TT * (b + 1))
                for k in range(KC):
                    if b == 1 and k == KC - 1:
                        pe.wait_ge(h_ready, 1)
                    for i in range(TT):
                        last = pe.transpose(ln_banks[b][k][:, i * P:(i + 1) * P],
                                            acc[:, TT * b + i, k * P:(k + 1) * P], ident[:, :])
                    last.then_inc(x_turned, 1)
            pe.wait_ge(mod_read, 1)
            pe.wait_ge(h_lo, KC)
            project_k(0, 0, 0)
            pe.wait_ge(h_ready, B * KC)
            project_q(0, 0)
            pe.wait_ge(k_rot, 1)
            project_v(0, 0, 0)
            project_q(0, 1)
            turn_v(0, 0)
            pe.wait_ge(h_lo, B * KC)

            group(0, first=True)
            with pe.Fori(1, KV - 1) as g:
                group(g)
            group(KV - 1, last=True)

            turn_probs(KV - 1, STEPS - 1, final=True)
            def turn_f(u, src):
                if u >= 2:
                    pe.wait_ge(f_lo, u - 1)
                for i in range(4):
                    last = pe.transpose((q_bank, x_bank)[u % 2][:, i * P:(i + 1) * P], src(i), ident[:, :])
                last.then_inc(f_turned, 1)

            pe.wait_ge(w12_in, 32)
            for u in range(KC):
                turn_f(u, lambda i: wq_raw[:, i, u * P:(u + 1) * P])
            attend(KV - 1, STEPS - 1)
            for u in range(KC):
                turn_f(KC + u, lambda i: wo_raw[:, i, u * P:(u + 1) * P])
            pe.wait_ge(pT_lo, 3 * STEPS * KV)
            out_banks = [s_row1, s_row20, s_row3, t_col0]
            for i in range(TT):
                project_out(KV - 1, 1, i, out_banks[i][:, :])
            pe.wait_ge(w3_in, 16)
            for u in range(4):
                turn_f(2 * KC + u, lambda i: wq_raw[:, i, u * P:(u + 1) * P])
            for a in range(2):
                for b in range(B):
                    pe.wait_ge(gate_wide, B * a + b + 1)
                    if B * a + b >= 1:
                        pe.wait_ge(gate_copied, B * a + b)
                    for k in range(KC):
                        last = pe.transpose(o_bank[:, k * P:(k + 1) * P], xn2[:, k, 0:P], ident[:, :])
                    last.then_inc(gate_turned, 1)

            pe.wait_ge(f_lo, 3 * KC)
            pe.wait_ge(gate_copied, 2 * B)
            for b in range(B):
                pe.wait_ge(x1_normed, TT * (b + 1))
                if b == 1:
                    pe.wait_ge(y_made, TT)
                for k in range(KC):
                    for i in range(TT):
                        last = pe.transpose(h2_banks[k][:, i * P:(i + 1) * P], xn2[:, i, k * P:(k + 1) * P], ident[:, :])
                    last.then_inc(h2_turned, 1)
                pe.wait_ge(h2_lo, KC * (b + 1))
                if b == 0:
                    pe.wait_ge(wo_added, STEPS * KV)
                for m in range(FF // P):
                    if TT * b + m >= 2:
                        pe.wait_ge(x4_made, TT * b + m - 1)
                    for half in range(2):
                        col = half * FF + m * P
                        product(up_banks[2 * (m % 2) + half][:, :], lambda a, k: w12T[a][:, k, col:col + P],
                                lambda a, k: h2T[a][:, REP * b + k, :], range(KC)).then_inc(up_made, 1)
                pe.wait_ge(x4_lo, KC * (b + 1))
                for i in range(TT):
                    product(h2_banks[i][:, :], lambda a, m: x4_at(a, b, m)[:, i * P:(i + 1) * P],
                            lambda a, m: w3T[a][:, m, :], range(FF // P)).then_inc(down_made, 1)

        @block.vector
        def _(dve):
            chain = [0]

            def link(ins):
                chain[0] += 1
                ins.then_inc(dve_chain, 1)
                dve.wait_ge(dve_chain, chain[0])

            half = HD // 2

            def rotate(src, cos_part, sin_part):
                nc.vector.tensor_tensor(cos_part, src[:, :], cos_sb[:, :], ALU.mult)
                nc.vector.tensor_tensor(sin_part[0:half, :], src[half:HD, :], sin_sb[half:HD, :], ALU.mult)
                return nc.vector.tensor_tensor(sin_part[half:HD, :], src[0:half, :], sin_sb[0:half, :], ALU.mult)

            def rotate_k(g, m_off):
                need(dve, k_lo, 2, g, m_off)
                need(dve, k_proj, 2, g, m_off + 1)
                rotate(x_bank, k_tmp[:, 0, :], k_tmp[:, 1, :]).then_inc(k_rot, 1)

            def rotate_q(g, j):
                need(dve, q_lo, STEPS, g, j - 1)
                need(dve, q_proj, STEPS, g, j + 1)
                rotate(q_bank, q_tmp[:, j % 2, 0, :], q_tmp[:, j % 2, 1, :]).then_inc(q_rot, 1)

            def maxima(g, j):
                s = j % 2
                need(dve, pT_turned, 3 * STEPS, g, 3 * (j - 1))
                for k, tiles in enumerate(((1,), (2, 0), (3,))):
                    need(dve, scores_ready, 3 * STEPS, g, 3 * j + k + 1)
                    nc.vector.memset(wait_mark[:, s, k:k + 1], 0.0)
                    for i in tiles:
                        last = nc.vector.tensor_tensor_reduce(
                            probs[:, s, ROW_AT[i]:ROW_AT[i] + ROW_W[i]], s_out[i], mask_sb[:, T - ROW_W[i]:T],
                            1.0, LOWEST, ALU.add, ALU.max, row_max[:, s, i:i + 1])
                    last.then_inc(rows_maxed, 1)
                need(dve, rows_maxed, 3 * STEPS, g, 3 * j + 3)
                nc.vector.tensor_scalar(neg_max[:, s, :], row_max[:, s, :], -SCALE, None, ALU.mult).then_inc(negmax_ready, 1)

            def normalise(g, j):
                s = j % 2
                need(dve, exp_done, STEPS, g, j + 1)
                nc.vector.reciprocal(row_inv[:, s, :], row_sum[:, s, :]).then_inc(inv_ready, 1)
                need(dve, inv_ready, STEPS, g, j + 1)
                for i in range(TT):
                    span = probs[:, s, ROW_AT[i]:ROW_AT[i] + ROW_W[i]]
                    last = nc.vector.tensor_scalar(span, span, row_inv[:, s, i:i + 1], None, ALU.mult)
                last.then_inc(probs_normed, 1)

            def probs_low(g, j):
                for k, (lo, hi) in enumerate(T_BANKS):
                    need(dve, pT_hi, 3 * STEPS, g, 3 * j + k + 1)
                    nc.vector.tensor_tensor(pT[1][:, lo:hi], t_banks[k], pT[0][:, lo:hi].bitcast(f32),
                                            ALU.subtract).then_inc(pT_lo, 1)

            def attn_low(g, j):
                need(dve, attn_hi, STEPS, g, j + 1)
                s = j % STEPS
                nc.vector.tensor_tensor(attn[1][:, s, :], o_bank[:, :], attn[0][:, s, :].bitcast(f32),
                                        ALU.subtract).then_inc(attn_lo, 1)

            def v_low(g, b, m_off):
                need(dve, v_hi, 2, g, m_off + 1)
                nc.vector.tensor_tensor(v_flat[1][:, b, :], x_bank[:, :], v_flat[0][:, b, :].bitcast(f32),
                                        ALU.subtract).then_inc(v_lo, 1)

            def add_out(g, w, w_off, first=False, src=None):
                src = x_bank if src is None else src
                need(dve, wo_made, STEPS, g, w_off + 1)
                if first:
                    nc.vector.tensor_copy(acc[:, w, :], src[:, :]).then_inc(wo_added, 1)
                else:
                    nc.vector.tensor_tensor(acc[:, w, :], src[:, :], acc[:, w, :], ALU.add).then_inc(wo_added, 1)

            def group(g, first=False, last=False):
                for j in range(STEPS):
                    maxima(g, j)
                    if not (first and j == 0):
                        probs_low(g, j - 1)
                    if not (last and j + 2 >= STEPS):
                        rotate_q(g, j + 2)
                    normalise(g, j)
                    if j == 0:
                        rotate_k(g, 1)
                    if j == 4 and not last:
                        rotate_k(g, 2)
                    if j in (1, 2) and not first:
                        add_out(g, TT + 2 * (j - 1), -TT + 2 * (j - 1))
                    if j in (5, 6):
                        add_out(g, 2 * (j - 5), 2 * (j - 5), first=first)
                    if first and j == 2:
                        dve.wait_ge(mod_made, 4)
                        nc.vector.tensor_copy(mod[:, 2 * KC:6 * KC, :].rearrange("p m b -> p (m b)"),
                                              x_bank[:, 4 * KC:12 * KC]).then_inc(mod_read, 1)
                        dve.wait_ge(mod_read, 2)
                        nc.vector.memset(acc[:, TT:2 * TT, :], 0.0)
                        nc.vector.tensor_scalar(one_plus[:, KC:2 * KC, :], mod[:, 4 * KC:5 * KC, :], 1.0, None, ALU.add)
                        for a, m in enumerate((2, 5)):
                            src = mod[:, m * KC:(m + 1) * KC, :]
                            sign = gate_sign[:, a * KC:(a + 1) * KC, :]
                            size = gate[:, a * KC:(a + 1) * KC, :]
                            link(nc.vector.tensor_scalar(sign, src, 0.0, 2.0, ALU.is_ge, ALU.mult))
                            link(nc.vector.tensor_scalar(sign, sign, -1.0, None, ALU.add))
                            link(nc.vector.tensor_tensor(size, src, sign, ALU.mult))
                            link(nc.vector.tensor_scalar(size, size, 0.25, None, ALU.max))
                            link(nc.vector.tensor_tensor(size, size, sign, ALU.mult))
                    if not (first and j == 0):
                        attn_low(g, j - 1)
                    if j in (1, 2) and not first:
                        add_out(g, TT + 2 * (j - 1) + 1, -TT + 2 * (j - 1) + 1)
                    if j in (5, 6):
                        add_out(g, 2 * (j - 5) + 1, 2 * (j - 5) + 1, first=first)
                    if j == 3:
                        v_low(g, 1, 1)
                    if j == 7 and not last:
                        v_low(g, 0, 2)

            def layer_norm_stats(w, src):
                link(nc.vector.bn_stats(stats[:, w, :], src))
                nc.vector.bn_aggr(moments[:, w, :], stats[:, w, :]).then_inc(moments_ready, 1)

            def norm_scale(b, done):
                dve.wait_ge(moments_ready, done)
                w = slice(TT * b, TT * (b + 1))
                v, y, t = var_eps[:, w, :], rstd[:, w, :], newton[:, w, :]
                link(nc.vector.tensor_scalar(v, moments[:, w, 1:2], EPS, None, ALU.add))
                link(nc.vector.tensor_scalar(y.bitcast(i32), v.bitcast(i32), -0.5, float(0x5f3759df), ALU.mult, ALU.add))
                for _ in range(3):
                    link(nc.vector.tensor_tensor(t, y, y, ALU.mult))
                    link(nc.vector.tensor_tensor(t, t, v, ALU.mult))
                    link(nc.vector.tensor_scalar(t, t, -0.5, 1.5, ALU.mult, ALU.add))
                    link(nc.vector.tensor_tensor(y, y, t, ALU.mult))

            dve.wait_ge(c_exped, 1)
            link(nc.vector.tensor_scalar(c_exp[:, :, :], c_exp[:, :, :], 1.0, None, ALU.add))
            link(nc.vector.reciprocal(c_silu[:, :, :], c_exp[:, :, :]))
            nc.vector.tensor_tensor(c_silu[:, :, :], c_silu[:, :, :], cT[:, :, :], ALU.mult).then_inc(c_ready, 1)

            def norm_x(b):
                dve.wait_ge(x_in[b], 16)
                for w in range(TT * b, TT * (b + 1)):
                    layer_norm_stats(w, acc[:, w, :])
                norm_scale(b, TT * (b + 1))
                for w in range(TT * b, TT * (b + 1)):
                    nc.vector.tensor_scalar(acc[:, w, :], acc[:, w, :], moments[:, w, 0:1], rstd[:, w, :],
                                            ALU.subtract, ALU.mult).then_inc(x_normed, 1)

            def modulate_x(b):
                for k in range(KC):
                    u = KC * b + k
                    dve.wait_ge(x_turned, u + 1)
                    if u >= 2:
                        dve.wait_ge(h_lo, u - 1)
                    nc.vector.tensor_scalar(k_tmp[:, u % 2, :], ln_banks[b][k][:, :], one_plus[:, k, b:b + 1],
                                            mod[:, k, b:b + 1], ALU.mult, ALU.add).then_inc(h_ready, 1)

            norm_x(0)
            norm_x(1)
            dve.wait_ge(mod_made, 2)
            nc.vector.tensor_copy(mod[:, 0:2 * KC, :].rearrange("p m b -> p (m b)"),
                                  x_bank[:, 0:4 * KC]).then_inc(mod_read, 1)
            dve.wait_ge(mod_read, 1)
            link(nc.vector.tensor_scalar(one_plus[:, 0:KC, :], mod[:, KC:2 * KC, :], 1.0, None, ALU.add))
            modulate_x(0)
            modulate_x(1)
            dve.wait_ge(h_lo, B * KC)
            rotate_k(0, 0)
            rotate_q(0, 0)
            rotate_q(0, 1)
            v_low(0, 0, 0)

            group(0, first=True)
            with dve.Fori(1, KV - 1) as g:
                group(g)
            group(KV - 1, last=True)

            probs_low(KV - 1, STEPS - 1)

            def f_low(u):
                dve.wait_ge(f_hi, u + 1)
                dst, bnk = f_place(u), (q_bank, x_bank)[u % 2]
                nc.vector.tensor_tensor(dst[1], bnk[:, :], dst[0].bitcast(f32), ALU.subtract).then_inc(f_lo, 1)

            for u in range(KC):
                f_low(u)
            attn_low(KV - 1, STEPS - 1)
            for u in range(KC, 2 * KC):
                f_low(u)
            for i, src in enumerate([s_row1, s_row20, s_row3, t_col0]):
                add_out(KV - 1, TT + i, TT + i, src=src)
            for u in range(2 * KC, 3 * KC):
                f_low(u)
            for a in range(2):
                for b in range(B):
                    if B * a + b >= 1:
                        dve.wait_ge(gate_turned, B * a + b)
                    for k in range(KC):
                        last = nc.vector.tensor_scalar(xn2[:, k, 0:P], ident[:, :], 0.0, gate[:, a * KC + k, b:b + 1],
                                                       ALU.mult, ALU.add)
                    last.then_inc(gate_wide, 1)
            dve.wait_ge(gate_copied, 2 * B)
            dve.wait_ge(b3_in, 16)

            def second_norm(b):
                for w in range(TT * b, TT * (b + 1)):
                    link(nc.vector.tensor_tensor(acc[:, w, :], acc[:, w, :], gate_w[0][b], ALU.mult))
                    dve.wait_ge(xr_in[w % 2], 16 * (w // 2 + 1))
                    nc.vector.tensor_tensor(acc[:, w, :], acc[:, w, :], x_ring[w % 2], ALU.add).then_inc(x_used, 1)
                    dve.wait_ge(x_used, w + 1)
                    layer_norm_stats(w, acc[:, w, :])
                norm_scale(b, TT * (B + b + 1))
                for w in range(TT * b, TT * (b + 1)):
                    if b == 1:
                        dve.wait_ge(h2_turned, KC)
                    nc.vector.tensor_scalar(xn2[:, w % TT, :], acc[:, w, :], moments[:, w, 0:1], rstd[:, w, :],
                                            ALU.subtract, ALU.mult).then_inc(x1_normed, 1)

            def modulate_x1(b):
                for k in range(KC):
                    u = KC * b + k
                    dve.wait_ge(h2_turned, u + 1)
                    if u >= 2:
                        dve.wait_ge(h2_lo, u - 1)
                    nc.vector.tensor_scalar(h2_tmp[:, u % 2, :], h2_banks[k][:, :], one_plus[:, KC + k, b:b + 1],
                                            mod[:, 3 * KC + k, b:b + 1], ALU.mult, ALU.add).then_inc(h2_ready, 1)

            def gate_up(b):
                for m in range(FF // P):
                    u = TT * b + m
                    e, r = up_tmp[u % 2]
                    x1b, x2b = up_banks[2 * (m % 2)], up_banks[2 * (m % 2) + 1]
                    dve.wait_ge(e_made, u + 1)
                    link(nc.vector.tensor_scalar(e, e, 1.0, None, ALU.add))
                    link(nc.vector.reciprocal(r, e))
                    link(nc.vector.scalar_tensor_tensor(out=e, in0=x1b[:, :], scalar=b12T[:, m:m + 1], in1=r,
                                                        op0=ALU.add, op1=ALU.mult))
                    dve.wait_ge(up_made, 2 * (u + 1))
                    nc.vector.scalar_tensor_tensor(out=r, in0=x2b[:, :], scalar=b12T[:, KC + m:KC + m + 1], in1=e,
                                                   op0=ALU.add, op1=ALU.mult).then_inc(x4_made, 1)

            def finish(b):
                for i in range(TT):
                    w = TT * b + i
                    tmp = up_tmp[i % 2][0]
                    dve.wait_ge(down_made, w + 1)
                    link(nc.vector.tensor_tensor(tmp, h2_banks[i][:, :], b3_w, ALU.add))
                    link(nc.vector.tensor_tensor(tmp, tmp, gate_w[1][b], ALU.mult))
                    nc.vector.tensor_tensor(acc[:, w, :], acc[:, w, :], tmp, ALU.add).then_inc(y_made, 1)

            second_norm(0)
            modulate_x1(0)
            second_norm(1)
            gate_up(0)
            finish(0)
            modulate_x1(1)
            gate_up(1)
            finish(1)

        @block.scalar
        def _(act):
            def split_hi(dst, src, done):
                nc.scalar.activation(dst, src, ACT.Copy).then_inc(done, 1)

            def wq_high(g, h, g_off):
                need(act, wq_in, 16, g, 16 * (g_off + 1))
                need(act, q_proj, STEPS, g, STEPS * g_off - REP + h + 1)
                split_hi(wq_s[0][:, h, :, :], wq_raw[:, :, h * HD:(h + 1) * HD], wq_hi)

            def wk_high(g, g_off):
                need(act, wk_in, 16, g, 16 * (g_off + 1))
                need(act, k_proj, 2, g, 2 * g_off)
                split_hi(wk_s[0][:, :, :], wk_raw[:, :, :], wk_hi)

            def wv_high(g, g_off):
                need(act, wv_in, 16, g, 16 * (g_off + 1))
                need(act, v_proj, 2, g, 2 * g_off)
                split_hi(wv_s[0][:, :, :], wv_raw[:, :, :], wv_hi)

            def wo_high(g, r, first):
                need(act, wo_in, 16, g, 16)
                need(act, wo_made, STEPS, g, 0)
                if first:
                    act.wait_ge(mod_made, 4)
                split_hi(wo_s[0][:, r, :], wo_raw[:, r, :], wo_hi)

            def probs_high(g, j):
                need(act, attn_done, STEPS, g, j)
                for k, (lo, hi) in enumerate(T_BANKS):
                    need(act, pT_turned, 3 * STEPS, g, 3 * j + k + 1)
                    split_hi(pT[0][:, lo:hi], t_banks[k], pT_hi)

            def exponents(g, j):
                s = j % 2
                need(act, negmax_ready, STEPS, g, j + 1)
                for i in range(TT):
                    span = probs[:, s, ROW_AT[i]:ROW_AT[i] + ROW_W[i]]
                    last = nc.scalar.activation(span, span, ACT.Exp, bias=neg_max[:, s, i:i + 1], scale=SCALE,
                                                accum_out=row_sum[:, s, i:i + 1])
                last.then_inc(exp_done, 1)

            def q_high(g, j):
                need(act, scores_ready, 3 * STEPS, g, 3 * (j - 1))
                need(act, q_sum, STEPS, g, j + 1)
                split_hi(qT[0][:, j % 2, :], q_tmp[:, j % 2, 0, :], q_hi)

            def k_high(g, b, m_off):
                need(act, scores_ready, 3 * STEPS, g, 3 * REP * (m_off - 1))
                need(act, k_sum, 2, g, m_off + 1)
                split_hi(kT[0][:, b, :], k_tmp[:, 0, :], k_hi)

            def v_copy(g, m_off):
                need(act, v_turned, 2, g, m_off)
                need(act, v_proj, 2, g, m_off + 1)
                split_hi(vT[:, :], x_bank[:, :], v_copied)

            def v_high(g, b, m_off):
                need(act, attn_done, STEPS, g, REP * (m_off - 1))
                need(act, v_turned, 2, g, m_off + 1)
                split_hi(v_flat[0][:, b, :], x_bank[:, :], v_hi)

            def attn_high(g, j):
                need(act, attn_done, STEPS, g, j + 1)
                if j >= 0:
                    need(act, wo_made, STEPS, g, TT * (j // REP - 1))
                split_hi(attn[0][:, j % STEPS, :], o_bank[:, :], attn_hi)

            def group(g, first=False, last=False):
                for j in range(STEPS):
                    if not (first and j == 0):
                        probs_high(g, j - 1)
                    exponents(g, j)
                    if not (last and j + 2 >= STEPS):
                        q_high(g, j + 2)
                    if j == 3:
                        v_copy(g, 1)
                    if j == 7 and not last:
                        v_copy(g, 2)
                    if not (first and j == 0):
                        attn_high(g, j - 1)
                    if j == 0:
                        k_high(g, 1, 1)
                    if j == 4 and not last:
                        k_high(g, 0, 2)
                    if j == 3:
                        v_high(g, 1, 1)
                    if j == 7 and not last:
                        v_high(g, 0, 2)
                    if j == 1 and not last:
                        wk_high(g, 1)
                    if j == 5 and not last:
                        wv_high(g, 1)
                    if 3 <= j <= 6 and not last:
                        wq_high(g, j - 3, 1)
                    if j in (3, 4):
                        for r in range(2 * (j - 3), 2 * (j - 3) + 2):
                            wo_high(g, r, first)

            act.dma_start(cT[:, :, 0], c[0, :].rearrange("(k p) -> p k", p=P), allow_slow_non_contiguous=True).then_inc(c_in, 16)
            act.dma_start(cT[:, :, 1], c[1, :].rearrange("(k p) -> p k", p=P), allow_slow_non_contiguous=True).then_inc(c_in, 16)
            for dst, src in ((ident, ident_t), (cos_sb, cos_t), (sin_sb, sin_t), (mask_sb, mask_t)):
                act.dma_start(dst[:, :], src).then_inc(tables_in, 16)
            act.dma_start(b12T[:, :], b12.rearrange("(m p) -> p m", p=P), allow_slow_non_contiguous=True).then_inc(b_in, 16)
            act.wait_ge(c_in, 32)
            nc.scalar.activation(c_exp[:, :, :], cT[:, :, :], ACT.Exp, scale=-1.0).then_inc(c_exped, 1)
            act.wait_ge(b_in, 16)
            nc.scalar.activation(neg_b1[:, :], b12T[:, 0:KC], ACT.Copy, scale=-1.0)
            wk_high(0, 0)
            for u in range(B * KC):
                if u == KC:
                    wq_high(0, 0, 0)
                b, k = u // KC, u % KC
                act.wait_ge(h_ready, u + 1)
                split_hi(hT[0][:, k, b * T:(b + 1) * T], k_tmp[:, u % 2, :], h_hi)
            wv_high(0, 0)
            for h in range(1, REP):
                wq_high(0, h, 0)
            k_high(0, 0, 0)
            q_high(0, 0)
            v_copy(0, 0)
            q_high(0, 1)
            v_high(0, 0, 0)

            group(0, first=True)
            with act.Fori(1, KV - 1) as g:
                group(g)
            group(KV - 1, last=True)

            probs_high(KV - 1, STEPS - 1)

            def f_high(u):
                act.wait_ge(f_turned, u + 1)
                split_hi(f_place(u)[0], (q_bank, x_bank)[u % 2][:, :], f_hi)

            for u in range(KC):
                f_high(u)
            attn_high(KV - 1, STEPS - 1)
            for u in range(KC, 3 * KC):
                f_high(u)
            act.wait_ge(pT_turned, 3 * STEPS * KV)
            act.dma_start(b3_w, b3.rearrange("(a n) -> a n", a=1).to_broadcast([P, HID])).then_inc(b3_in, 16)
            for a in range(2):
                for b in range(B):
                    act.wait_ge(gate_turned, B * a + b + 1)
                    split_hi(gate_w[a][b], o_bank[:, :], gate_copied)

            for b in range(B):
                for k in range(KC):
                    u = KC * b + k
                    act.wait_ge(h2_ready, u + 1)
                    split_hi(h2T[0][:, REP * b + k, :], h2_tmp[:, u % 2, :], h2_hi)
                for m in range(FF // P):
                    u = TT * b + m
                    act.wait_ge(up_made, 2 * u + 1)
                    if u >= 2:
                        act.wait_ge(x4_lo, u - 1)
                    if b == 1 and m < 2:
                        act.wait_ge(y_made, TT)
                    nc.scalar.activation(up_tmp[u % 2][0], up_banks[2 * (m % 2)][:, :], ACT.Exp,
                                         bias=neg_b1[:, m:m + 1], scale=-1.0).then_inc(e_made, 1)
                    act.wait_ge(x4_made, u + 1)
                    split_hi(x4_at(0, b, m), up_tmp[u % 2][1], x4_hi)

        @block.gpsimd
        def _(pool):
            def split_lo(dst, src, hi, done):
                nc.gpsimd.tensor_tensor(dst, src, hi.bitcast(f32), ALU.subtract).then_inc(done, 1)

            def wq_low(g, h, g_off):
                need(pool, wq_hi, REP, g, REP * g_off + h + 1)
                split_lo(wq_s[1][:, h, :, :], wq_raw[:, :, h * HD:(h + 1) * HD], wq_s[0][:, h, :, :], wq_lo)

            def wk_low(g, g_off):
                need(pool, wk_hi, 1, g, g_off + 1)
                split_lo(wk_s[1][:, :, :], wk_raw[:, :, :], wk_s[0][:, :, :], wk_lo)

            def wv_low(g, g_off):
                need(pool, wv_hi, 1, g, g_off + 1)
                split_lo(wv_s[1][:, :, :], wv_raw[:, :, :], wv_s[0][:, :, :], wv_lo)

            def wo_low(g, r):
                need(pool, wo_hi, REP, g, r + 1)
                split_lo(wo_s[1][:, r, :], wo_raw[:, r, :], wo_s[0][:, r, :], wo_lo)

            def q_add(g, j):
                need(pool, q_rot, STEPS, g, j + 1)
                s = j % 2
                nc.gpsimd.tensor_tensor(q_tmp[:, s, 0, :], q_tmp[:, s, 0, :], q_tmp[:, s, 1, :], ALU.add).then_inc(q_sum, 1)

            def q_low(g, j):
                need(pool, q_hi, STEPS, g, j + 1)
                split_lo(qT[1][:, j % 2, :], q_tmp[:, j % 2, 0, :], qT[0][:, j % 2, :], q_lo)

            def k_add(g, m_off):
                need(pool, k_rot, 2, g, m_off + 1)
                nc.gpsimd.tensor_tensor(k_tmp[:, 0, :], k_tmp[:, 0, :], k_tmp[:, 1, :], ALU.add).then_inc(k_sum, 1)

            def k_low(g, b, m_off):
                need(pool, k_hi, 2, g, m_off + 1)
                split_lo(kT[1][:, b, :], k_tmp[:, 0, :], kT[0][:, b, :], k_lo)

            def group(g, first=False, last=False):
                for j in range(STEPS):
                    if not (last and j + 2 >= STEPS):
                        q_add(g, j + 2)
                        q_low(g, j + 2)
                    if j == 0:
                        k_add(g, 1)
                        k_low(g, 1, 1)
                    if j == 4 and not last:
                        k_add(g, 2)
                        k_low(g, 0, 2)
                    if j == 1 and not last:
                        wk_low(g, 1)
                    if j == 5 and not last:
                        wv_low(g, 1)
                    if 3 <= j <= 6 and not last:
                        wq_low(g, j - 3, 1)
                    if j in (3, 4):
                        for r in range(2 * (j - 3), 2 * (j - 3) + 2):
                            wo_low(g, r)

            wk_low(0, 0)
            for u in range(B * KC):
                if u == KC:
                    wq_low(0, 0, 0)
                b, k = u // KC, u % KC
                pool.wait_ge(h_hi, u + 1)
                at = slice(b * T, (b + 1) * T)
                split_lo(hT[1][:, k, at], k_tmp[:, u % 2, :], hT[0][:, k, at], h_lo)
            wv_low(0, 0)
            for h in range(1, REP):
                wq_low(0, h, 0)
            k_add(0, 0)
            k_low(0, 0, 0)
            q_add(0, 0)
            q_low(0, 0)
            q_add(0, 1)
            q_low(0, 1)

            group(0, first=True)
            with pool.Fori(1, KV - 1) as g:
                group(g)
            group(KV - 1, last=True)

            for b in range(B):
                for k in range(KC):
                    u = KC * b + k
                    pool.wait_ge(h2_hi, u + 1)
                    split_lo(h2T[1][:, REP * b + k, :], h2_tmp[:, u % 2, :], h2T[0][:, REP * b + k, :], h2_lo)
                for m in range(FF // P):
                    u = TT * b + m
                    pool.wait_ge(x4_hi, u + 1)
                    split_lo(x4_at(1, b, m), up_tmp[u % 2][1], x4_at(0, b, m), x4_lo)


def rope_tables():
    theta, factor, hi_ff, lo_ff, orig_max = 500000.0, 8.0, 4.0, 1.0, 1024
    inv = 1.0 / theta ** (np.arange(0, HD, 2, dtype=np.float64) / HD)
    wavelen = 2.0 * np.pi / inv
    smooth = (orig_max / wavelen - lo_ff) / (hi_ff - lo_ff)
    scaled = np.where(wavelen > orig_max / lo_ff, inv / factor, inv)
    mid = (wavelen <= orig_max / lo_ff) & (wavelen >= orig_max / hi_ff)
    scaled = np.where(mid, (1 - smooth) * inv / factor + smooth * inv, scaled).astype(np.float32)
    freqs = np.arange(T, dtype=np.float32)[:, None] * scaled[None, :]
    cos, sin = np.cos(freqs).T, np.sin(freqs).T
    return (np.ascontiguousarray(np.concatenate([cos, cos])).astype(np.float32),
            np.ascontiguousarray(np.concatenate([sin, -sin])).astype(np.float32))


def causal_mask():
    mask = np.zeros((P, T), np.float32)
    mask[:, T - P:][np.triu_indices(P, 1)] = MASKED
    return mask


_INS = ['L0_attn_x', 'L0_attn_wq', 'L0_attn_wk', 'L0_attn_wv', 'L0_attn_wo', 'L0_ffn_w12', 'L0_ffn_b12',
        'L0_ffn_w3', 'L0_ffn_b3', 'L0_c', 'L0_wmod']


def kernel(**inputs):
    import concourse.bacc as _bacc
    from concourse.bass_utils import run_bass_kernel_spmd as _run

    nc = _bacc.Bacc("TRN2", target_bir_lowering=False, num_devices=1)
    cos, sin = rope_tables()
    given = [(n, np.ascontiguousarray(inputs[n])) for n in _INS]
    given += [("rope_cos", cos), ("rope_sin", sin), ("causal_mask", causal_mask()),
              ("identity", np.eye(P, dtype=np.float32))]
    arrays, args = {}, []
    for name, a in given:
        arrays[f"in_{name}_dram"] = a
        args.append(nc.dram_tensor(f"in_{name}_dram", a.shape, mybir.dt.from_np(a.dtype), kind="ExternalInput").ap())
    args.append(nc.dram_tensor("out_dram", (B, T, HID), mybir.dt.float32, kind="ExternalOutput").ap())
    adaln_block(nc, *args)
    r = _run(nc, [arrays], core_ids=[0])
    return r.results[0]["out_dram"]
```

```python
import concourse.bass as bass
from concourse import mybir
from contextlib import ExitStack
import numpy as np

B, T, HID = 2, 512, 512
H, KV, HD = 32, 8, 128
FF = 512
P = 128
TT = T // P
KC = HID // P
REP = H // KV
STEPS = B * REP
EPS = 1e-5
SCALE = 1.0 / float(np.sqrt(HD))
MASKED = -1.0e30
LOWEST = -3.0e38

ROW_W = [P * (i + 1) for i in range(TT)]
ROW_AT = [sum(ROW_W[:i]) for i in range(TT)]
ROWS = sum(ROW_W)
COL_W = [T - P * j for j in range(TT)]
COL_AT = {0: 0, 1: COL_W[0], 3: COL_W[0] + COL_W[1], 2: COL_W[0] + COL_W[1] + COL_W[3]}
T_BANKS = [(0, T), (T, 2 * T), (2 * T, ROWS)]


def adaln_block(nc, x, wq, wk, wv, wo, w12, b12, w3, b3, c, wmod, cos_t, sin_t, mask_t, ident_t, out):
    f32, f32r, i32 = mybir.dt.float32, mybir.dt.float32r, mybir.dt.int32
    ALU, ACT = mybir.AluOpType, mybir.ActivationFunctionType

    x_tiles = x.rearrange("b (i p) f -> p (b i) f", p=P)
    out_tiles = out.rearrange("b (i p) f -> p (b i) f", p=P)
    wq_v = wq.rearrange("(k p) n -> p k n", p=P)
    wk_v = wk.rearrange("(k p) n -> p k n", p=P)
    wv_v = wv.rearrange("(k p) n -> p k n", p=P)
    wo_v = wo.rearrange("(h p) n -> p h n", p=P)
    wmod_v = wmod.rearrange("(p k) n -> p k n", p=P)
    w12_v = w12.rearrange("(m p) k -> p m k", p=P)
    w3_v = w3.rearrange("(n p) m -> p n m", p=P)

    st = ExitStack()
    with st:
        def sb(name, shape, dt=f32):
            return st.enter_context(nc.sbuf_tensor(name, shape, dt))

        def sem(name):
            return st.enter_context(nc.semaphore(name))

        cos_sb = sb("cos_sb", [P, T])
        sin_sb = sb("sin_sb", [P, T])
        mask_sb = sb("mask_sb", [P, T])
        ident = sb("ident", [P, P])
        acc = sb("acc", [P, B * TT, HID])
        wq_raw = sb("wq_raw", [P, KC, REP * HD])
        wk_raw = sb("wk_raw", [P, KC, HD])
        wv_raw = sb("wv_raw", [P, KC, HD])
        wo_raw = sb("wo_raw", [P, REP, HID])
        hT = [sb(f"hT_{s}", [P, KC, B * T], f32r) for s in ("hi", "lo")]
        wq_s = [sb(f"wq_{s}", [P, REP, KC, HD], f32r) for s in ("hi", "lo")]
        wk_s = [sb(f"wk_{s}", [P, KC, HD], f32r) for s in ("hi", "lo")]
        wv_s = [sb(f"wv_{s}", [P, KC, HD], f32r) for s in ("hi", "lo")]
        with nc.sbuf_tensor("wmod_sb", [P, 6, KC, HID], f32) as wmod_sb:
            pass
        wo_s = [sb(f"wo_{s}", [P, REP, HID], f32r) for s in ("hi", "lo")]
        attn = [sb(f"attn_{s}", [P, STEPS, T], f32r) for s in ("hi", "lo")]
        wmod_blocks = [wmod_sb[:, (m + 2) % 6, :, :] for m in range(6)]
        kT = [sb(f"kT_{s}", [P, B, T], f32r) for s in ("hi", "lo")]
        v_s = [sb(f"v_{s}", [P, B, TT, HD], f32r) for s in ("hi", "lo")]
        qT = [sb(f"qT_{s}", [P, 2, T], f32r) for s in ("hi", "lo")]
        pT = [sb(f"pT_{s}", [P, ROWS], f32r) for s in ("hi", "lo")]
        probs = sb("probs", [P, 2, ROWS])
        q_tmp = sb("q_tmp", [P, 2, 2, T])
        k_tmp = sb("k_tmp", [P, 2, T])
        vT = sb("vT", [P, T])
        cT = sb("cT", [P, B, KC])
        c_exp = sb("c_exp", [P, B, KC])
        c_silu = sb("c_silu", [P, B, KC])
        mod = sb("mod", [P, 6 * KC, B])
        one_plus = sb("one_plus", [P, 2 * KC, B])
        gate_sign = sb("gate_sign", [P, 2 * KC, B])
        gate = sb("gate", [P, 2 * KC, B])
        b12T = sb("b12T", [P, 2 * FF // P])
        neg_b1 = sb("neg_b1", [P, FF // P])
        stats = sb("stats", [P, B * TT, 6])
        moments = sb("moments", [P, B * TT, 2])
        rstd = sb("rstd", [P, B * TT, 1])
        var_eps = sb("var_eps", [P, B * TT, 1])
        newton = sb("newton", [P, B * TT, 1])
        shift = sb("shift", [P, B * TT, 1])
        wait_mark = sb("wait_mark", [P, 2, 3])
        row_max = sb("row_max", [P, 2, TT])
        neg_max = sb("neg_max", [P, 2, TT])
        row_sum = sb("row_sum", [P, 2, TT])
        row_inv = sb("row_inv", [P, 2, TT])

        def bank(name):
            return st.enter_context(nc.psum_tensor(name, [P, 512], f32))

        s_row1, s_row20, s_row3 = bank("s_row1"), bank("s_row20"), bank("s_row3")
        t_col0, t_col13 = bank("t_col0"), bank("t_col13")
        q_bank, x_bank, o_bank = bank("q_bank"), bank("x_bank"), bank("o_bank")
        s_out = [s_row20[:, ROW_W[2]:T], s_row1[:, 0:ROW_W[1]], s_row20[:, 0:ROW_W[2]], s_row3[:, :]]
        t_out = {0: t_col0[:, :], 1: t_col13[:, 0:COL_W[1]], 3: t_col13[:, COL_W[1]:T],
                 2: s_row1[:, T - COL_W[2]:T]}
        t_banks = [t_col0[:, :], t_col13[:, :], s_row1[:, T - COL_W[2]:T]]
        ln_banks = [[s_row1, s_row20, s_row3, t_col0], [t_col0, t_col13, t_col0, t_col13]]

        ident_in, tables_in, c_in, b_in = sem("ident_in"), sem("tables_in"), sem("c_in"), sem("b_in")
        x_in, wmod_in, wq0_in = [sem(f"x_in{i}") for i in range(3)], [sem(f"wmod_in{m}") for m in range(6)], sem("wq0_in")
        wq_in, wk_in, wv_in, wo_in = sem("wq_in"), sem("wk_in"), sem("wv_in"), sem("wo_in")
        wq_hi, wq_lo, wk_hi, wk_lo = sem("wq_hi"), sem("wq_lo"), sem("wk_hi"), sem("wk_lo")
        wv_hi, wv_lo, wo_hi, wo_lo = sem("wv_hi"), sem("wv_lo"), sem("wo_hi"), sem("wo_lo")
        dve_chain, zeros_made = sem("dve_chain"), sem("zeros_made")
        mod_rows, mod_rows_copied = sem("mod_rows"), sem("mod_rows_copied")
        c_exped, c_ready, mod_made, mod_read, mod_ready = (
            sem("c_exped"), sem("c_ready"), sem("mod_made"), sem("mod_read"), sem("mod_ready"))
        stats_made, moments_ready, norm_ready = sem("stats_made"), sem("moments_ready"), sem("norm_ready")
        x_normed, x_turned = sem("x_normed"), sem("x_turned")
        h_ready, h_hi, h_lo = ([sem(f"h_{s}{b}") for b in range(B)] for s in ("ready", "hi", "lo"))
        k_proj, k_copied, k_cos, k_sin, k_sum, k_hi, k_lo = (
            sem("k_proj"), sem("k_copied"), sem("k_cos"), sem("k_sin"), sem("k_sum"), sem("k_hi"), sem("k_lo"))
        v_proj, v_copied, v_turned, v_hi, v_lo = (
            sem("v_proj"), sem("v_copied"), sem("v_turned"), sem("v_hi"), sem("v_lo"))
        q_proj, q_copied, q_cos, q_sin, q_sum, q_hi, q_lo = (
            sem("q_proj"), sem("q_copied"), sem("q_cos"), sem("q_sin"), sem("q_sum"), sem("q_hi"), sem("q_lo"))
        scores_ready, rows_maxed, negmax_ready, exp_done = (
            sem("scores_ready"), sem("rows_maxed"), sem("negmax_ready"), sem("exp_done"))
        inv_ready, probs_normed = sem("inv_ready"), sem("probs_normed")
        pT_turned, pT_hi, pT_lo = sem("pT_turned"), sem("pT_hi"), sem("pT_lo")
        attn_done, attn_hi, attn_lo = sem("attn_done"), sem("attn_hi"), sem("attn_lo")
        wo_made, wo_added = sem("wo_made"), sem("wo_added")
        w12_in, w3_in = [sem(f"w12_in{i}") for i in range(2)], sem("w3_in")
        f_turned, f_hi, f_lo = sem("f_turned"), sem("f_hi"), sem("f_lo")
        gate_wide, gate_turned, gate_copied = sem("gate_wide"), sem("gate_turned"), sem("gate_copied")
        xr_in = [sem(f"xr_in{i}") for i in range(2)]
        x_gated, x1_made, x1_normed, h2_turned, h2_ready, h2_hi, h2_lo = (
            sem("x_gated"), sem("x1_made"), sem("x1_normed"), sem("h2_turned"), sem("h2_ready"),
            [sem(f"h2_hi{b}") for b in range(B)], [sem(f"h2_lo{b}") for b in range(B)])
        b3_in, gate_b3, x1_b3, up_made, e_made, x4_made, x4_hi, x4_lo = (
            sem("b3_in"), sem("gate_b3"), sem("x1_b3"), sem("up_made"), sem("e_made"), sem("x4_made"), sem("x4_hi"),
            sem("x4_lo"))
        down_made, down_gated, y_made, y_stored = sem("down_made"), sem("down_gated"), sem("y_made"), sem("y_stored")

        w12T = hT
        w3T = [w[:, :, :, :].rearrange("p r k d -> p r (k d)") for w in wq_s]
        h2T = attn
        k_flat = [k[:, :, :] for k in kT]
        v_flat = [v[:, :, :, :].rearrange("p b i d -> p b (i d)") for v in v_s]

        def x4_at(part, b, mc):
            if b == 1:
                return wo_s[part][:, mc, :]
            return (k_flat, v_flat)[mc // 2][part][:, mc % 2, :]

        xn2 = q_tmp[:, :, :, :].rearrange("p s c t -> p (s c) t")
        x_ring = [wk_raw[:, :, :].rearrange("p k d -> p (k d)"), wv_raw[:, :, :].rearrange("p k d -> p (k d)")]
        gate_w = [[k_tmp[:, 0, :], k_tmp[:, 1, :]], [cos_sb[:, :], sin_sb[:, :]]]
        b3_w = vT[:, :]
        gate_b3_w = [mask_sb[:, :], vT[:, :]]

        p_flat = probs[:, :, :].rearrange("p s n -> p (s n)")
        zeros = p_flat[:, KC * T:(KC + 1) * T]
        mod_row = [q_tmp[0:B, 0, m, :] for m in range(2)]
        mod_banks = [q_bank, t_col13]
        h2_tmp = [p_flat[:, k * T:(k + 1) * T] for k in range(KC)]
        h_tmp = [[p_flat[:, k * T:(k + 1) * T] for k in range(KC)], [k_tmp[:, k % 2, :] for k in range(KC)]]

        PARTS = [(0, 0), (0, 1), (1, 0)]

        def need(eng, s, per, g, off):
            if isinstance(g, int):
                if per * g + off > 0:
                    eng.wait_ge(s, per * g + off)
            elif per + off > 0:
                eng.wait_ge(s, g * per + off)
            else:
                assert per * (KV - 2) + off <= 0

        def head(j):
            return j // STEPS, j % STEPS // REP, j % REP

        ln2_banks = [[s_row20, s_row3, q_bank, x_bank], [t_col0, t_col13, s_row1, o_bank]]
        up_banks = [(s_row20, s_row3), (q_bank, x_bank)]
        out_banks = [t_col0, t_col13, s_row1, o_bank]
        up_tmp = [(wo_raw[:, 2 * i, :], wo_raw[:, 2 * i + 1, :]) for i in range(2)]
        y_tmp = [wq_raw[:, i, :] for i in range(TT)]
        f_banks = [q_bank] * 3 + [x_bank, q_bank] * 4 + [x_bank]
        f_before = [max([v for v in range(u) if f_banks[v] is f_banks[u]], default=None) for u in range(3 * KC)]

        def f_place(u):
            if u < 2 * KC:
                at = (u // KC) * FF
                return [w12T[s][:, u % KC, at:at + FF] for s in range(2)]
            return [w3T[s][:, u - 2 * KC, :] for s in range(2)]

        block = st.enter_context(nc.Block())

        @block.sync
        def _(sp):
            for i in range(2):
                sp.dma_start(acc[:, 2 * i:2 * i + 2, :], x_tiles[:, 2 * i:2 * i + 2, :]).then_inc(x_in[i], 16)

            def load_wmod(m):
                sp.dma_start(wmod_blocks[m], wmod_v[:, :, m * HID:(m + 1) * HID]).then_inc(wmod_in[m], 16)

            load_wmod(0)
            load_wmod(1)
            sp.dma_start(wk_raw[:, :, :], wk_v[:, :, 0:HD]).then_inc(wk_in, 16)
            sp.dma_start(wq_raw[:, :, 0:HD], wq_v[:, :, 0:HD]).then_inc(wq0_in, 16)
            sp.dma_start(acc[:, TT:2 * TT, :], x_tiles[:, TT:2 * TT, :]).then_inc(x_in[2], 16)
            for dst, src in ((cos_sb, cos_t), (sin_sb, sin_t), (mask_sb, mask_t)):
                sp.dma_start(dst[:, :], src).then_inc(tables_in, 16)
            sp.dma_start(wv_raw[:, :, :], wv_v[:, :, 0:HD]).then_inc(wv_in, 16)
            sp.dma_start(wq_raw[:, :, HD:REP * HD], wq_v[:, :, HD:REP * HD]).then_inc(wq_in, 16)
            for m in range(2, 6):
                load_wmod(m)
            sp.dma_start(wo_raw[:, :, :], wo_v[:, 0:REP, :]).then_inc(wo_in, 16)
            sp.dma_start(b12T[:, :], b12.rearrange("(m p) -> p m", p=P), allow_slow_non_contiguous=True).then_inc(b_in, 16)

            def next_weights(g):
                need(sp, wk_lo, 1, g, 1)
                sp.dma_start(wk_raw[:, :, :], wk_v[:, :, bass.ds((g + 1) * HD, HD)]).then_inc(wk_in, 16)
                need(sp, wq_lo, REP, g, REP)
                sp.dma_start(wq_raw[:, :, :], wq_v[:, :, bass.ds((g + 1) * (REP * HD), REP * HD)]).then_inc(wq_in, 16)
                need(sp, wv_lo, 1, g, 1)
                sp.dma_start(wv_raw[:, :, :], wv_v[:, :, bass.ds((g + 1) * HD, HD)]).then_inc(wv_in, 16)
                need(sp, wo_lo, REP, g, REP)
                sp.dma_start(wo_raw[:, :, :], wo_v[:, bass.ds((g + 1) * REP, REP), :]).then_inc(wo_in, 16)

            next_weights(0)
            with sp.Fori(1, KV - 1) as g:
                next_weights(g)
            sp.wait_ge(wq_lo, REP * KV)
            sp.dma_start(wq_raw[:, :, :], w12_v[:, 0:4, :]).then_inc(w12_in[0], 16)
            sp.wait_ge(wk_lo, KV)
            sp.dma_start(x_ring[0], x_tiles[:, 0, :]).then_inc(xr_in[0], 16)
            sp.wait_ge(wv_lo, KV)
            sp.dma_start(x_ring[1], x_tiles[:, 1, :]).then_inc(xr_in[1], 16)
            sp.wait_ge(wo_lo, REP * KV)
            sp.dma_start(wo_raw[:, :, :], w12_v[:, 4:8, :]).then_inc(w12_in[1], 16)
            sp.wait_ge(v_turned, 2 * KV)
            sp.dma_start(b3_w, b3.rearrange("(a n) -> a n", a=1).to_broadcast([P, HID])).then_inc(b3_in, 16)
            for w in range(2, B * TT):
                sp.wait_ge(x1_made, w - 1)
                sp.dma_start(x_ring[w % 2], x_tiles[:, w, :]).then_inc(xr_in[w % 2], 16)
                if w == 3:
                    sp.wait_ge(f_turned, KC)
                    sp.dma_start(wq_raw[:, :, :], w3_v).then_inc(w3_in, 16)
            for w in range(B * TT):
                sp.wait_ge(y_made, w + 1)
                sp.dma_start(out_tiles[:, w, :], acc[:, w, :]).then_inc(y_stored, 16)
            sp.wait_ge(y_stored, 16 * B * TT)

        @block.tensor
        def _(pe):
            def product(dst, lhs, rhs, chunks, chunk_ready=None):
                todo = [(cc, a, b) for cc in chunks for a, b in PARTS]
                for k, (cc, a, b) in enumerate(todo):
                    if chunk_ready is not None and k % len(PARTS) == 0:
                        pe.wait_ge(chunk_ready, cc + 1)
                    last = pe.matmul(dst, lhs(a, cc), rhs(b, cc), start=(k == 0), stop=(k == len(todo) - 1))
                return last

            def modulation(m, part, dst):
                pe.wait_ge(wmod_in[m], 16)
                for n in range(part * KC // 2, (part + 1) * KC // 2):
                    at = 2 * (KC * m + n)
                    for k in range(KC):
                        last = pe.matmul(dst[:, at:at + 2], wmod_blocks[m][:, k, n * P:(n + 1) * P],
                                         c_silu[:, :, k], start=(k == 0), stop=(k == KC - 1))
                last.then_inc(mod_made, 1)

            def project_k(g, b, m_off, chunk_ready=None):
                need(pe, wk_lo, 1, g, m_off // 2 + 1)
                product(x_bank[:, :], lambda a, k: wk_s[a][:, k, :],
                        lambda a, k: hT[a][:, k, b * T:(b + 1) * T], range(KC), chunk_ready).then_inc(k_proj, 1)

            def project_v(g, b, m_off):
                need(pe, wv_lo, 1, g, m_off // 2 + 1)
                product(x_bank[:, :], lambda a, k: wv_s[a][:, k, :],
                        lambda a, k: hT[a][:, k, b * T:(b + 1) * T], range(KC)).then_inc(v_proj, 1)

            def turn_v(g, m_off):
                need(pe, v_copied, 2, g, m_off + 1)
                for i in range(TT):
                    last = pe.transpose(x_bank[:, i * P:(i + 1) * P], vT[:, i * P:(i + 1) * P], ident[:, :])
                last.then_inc(v_turned, 1)

            def project_q(g, j):
                ahead, b, h = head(j)
                need(pe, q_copied, STEPS, g, j)
                need(pe, wq_lo, REP, g, REP * ahead + h + 1)
                product(q_bank[:, :], lambda a, k: wq_s[a][:, h, k, :],
                        lambda a, k: hT[a][:, k, b * T:(b + 1) * T], range(KC)).then_inc(q_proj, 1)

            def scores(g, j):
                _, b, h = head(j)
                need(pe, q_lo, STEPS, g, j + 1)
                if h == 0:
                    need(pe, k_lo, 2, g, b + 1)
                need(pe, rows_maxed, 3 * STEPS, g, 3 * j)
                need(pe, pT_lo, 3 * STEPS, g, 3 * (j - 1))
                for tiles in ((1,), (2, 0), (3,)):
                    for i in tiles:
                        last = product(s_out[i], lambda a, _: qT[a][:, j % 2, i * P:(i + 1) * P],
                                       lambda a, _: kT[a][:, b, 0:ROW_W[i]], [0])
                    last.then_inc(scores_ready, 1)

            def turn_probs(g, j, final=False):
                need(pe, probs_normed, STEPS, g, j + 1)
                need(pe, pT_lo, 3 * STEPS, g, 3 * j)
                for cols in ((0,), (1, 3), (2,)):
                    if cols == (2,):
                        need(pe, rows_maxed, 3 * STEPS, g, 3 * (j + 1) + (0 if final else 1))
                    for jj in cols:
                        for i in range(jj, TT):
                            at = ROW_AT[i] + jj * P
                            last = pe.transpose(t_out[jj][:, (i - jj) * P:(i - jj + 1) * P],
                                                probs[:, j % 2, at:at + P], ident[:, :])
                    last.then_inc(pT_turned, 1)

            def attend(g, j):
                _, b, h = head(j)
                need(pe, attn_lo, STEPS, g, j)
                if h == 0:
                    need(pe, v_lo, 2, g, b + 1)
                for k, cols in enumerate(((0,), (1, 3), (2,))):
                    need(pe, pT_lo, 3 * STEPS, g, 3 * j + k + 1)
                    for jj in cols:
                        for a, bb in PARTS:
                            last = pe.matmul(o_bank[:, jj * P:T], v_s[a][:, b, jj, :],
                                             pT[bb][:, COL_AT[jj]:COL_AT[jj] + COL_W[jj]],
                                             start=(jj == 0 and (a, bb) == PARTS[0]),
                                             stop=(jj == 2 and (a, bb) == PARTS[-1]))
                last.then_inc(attn_done, 1)

            def project_out(g, b, i, dst, g_off=0):
                need(pe, attn_lo, STEPS, g, STEPS * g_off + REP * (b + 1))
                need(pe, wo_lo, REP, g, REP * (g_off + 1))
                product(dst, lambda a, h: attn[a][:, REP * b + h, i * P:(i + 1) * P],
                        lambda a, h: wo_s[a][:, h, :], range(REP)).then_inc(wo_made, 1)

            def turn_gate(n, bank, src):
                pe.wait_ge(gate_wide, n + 1)
                for k in range(KC):
                    last = pe.transpose(bank[:, k * P:(k + 1) * P], src[:, k * P:(k + 1) * P], ident[:, :])
                last.then_inc(gate_turned, 1)

            def turn_f(u):
                if f_before[u] is not None:
                    pe.wait_ge(f_lo, f_before[u] + 1)
                src, rows = ((wq_raw, u), (wo_raw, u - KC), (wq_raw, u - 2 * KC))[u // KC]
                if u % KC == 0:
                    pe.wait_ge((*w12_in, w3_in)[u // KC], 16)
                for i in range(4):
                    last = pe.transpose(f_banks[u][:, i * P:(i + 1) * P], src[:, i, rows * P:(rows + 1) * P], ident[:, :])
                last.then_inc(f_turned, 1)

            def free_x_after_wo(g, w_off):
                need(pe, wo_added, STEPS, g, w_off)

            def group(g, first=False, last=False):
                for j in range(STEPS):
                    scores(g, j)
                    if first and j == 1:
                        need(pe, k_copied, 2, g, 2)
                        modulation(3, 0, x_bank)
                    if first and j == 2:
                        modulation(4, 1, x_bank)
                    if not (first and j == 0):
                        turn_probs(g, j - 1)
                    if first and j == 0:
                        turn_x(1, (2, 3))
                    if not (last and j + 2 >= STEPS):
                        project_q(g, j + 2)
                    if first and j == 0:
                        modulation(2, 0, o_bank)
                    if last and j == 6:
                        need(pe, q_copied, STEPS, g, STEPS)
                        turn_f(0)
                    if last and j == 7:
                        turn_f(2)
                    if j == 0:
                        need(pe, v_lo, 2, g, 1)
                        project_k(g, 1, 1, h_lo[1] if first else None)
                    if j in (1, 2) and not first:
                        if j == 1:
                            need(pe, k_copied, 2, g, 2)
                        free_x_after_wo(g, STEPS * 0 - TT + 2 * (j - 1))
                        project_out(g, 1, 2 * (j - 1), x_bank[:, :], g_off=-1)
                    if first and j == 0:
                        modulation(2, 1, o_bank)
                    if first and j == 1:
                        modulation(3, 1, x_bank)
                        pe.wait_ge(mod_read, 1)
                    if first and j == 2:
                        modulation(5, 0, x_bank)
                    if j == 3:
                        if first:
                            pe.wait_ge(mod_read, 2)
                        else:
                            free_x_after_wo(g, 0)
                        project_v(g, 1, 1)
                    if j == 4 and not last:
                        need(pe, v_lo, 2, g, 2)
                        project_k(g, 0, 2)
                    if j == 4 and last:
                        need(pe, v_lo, 2, g, 2)
                        turn_gate(0, x_bank, gate_w[0][0])
                    if j in (5, 6):
                        if j == 5 and not last:
                            need(pe, k_copied, 2, g, 3)
                        if j == 5 and last:
                            pe.wait_ge(gate_copied, 2)
                        free_x_after_wo(g, 2 * (j - 5))
                        project_out(g, 0, 2 * (j - 5), x_bank[:, :])
                    if j == 7 and not last:
                        free_x_after_wo(g, TT)
                        project_v(g, 0, 2)
                    if not (first and j == 0):
                        attend(g, j - 1)
                    if j in (1, 2) and not first:
                        free_x_after_wo(g, -TT + 2 * (j - 1) + 1)
                        project_out(g, 1, 2 * (j - 1) + 1, x_bank[:, :], g_off=-1)
                    if first and j == 1:
                        modulation(4, 0, x_bank)
                    if first and j == 2:
                        modulation(5, 1, x_bank)
                    if j == 3:
                        turn_v(g, 1)
                    if j == 4 and last:
                        pe.wait_ge(gate_copied, 1)
                        turn_gate(1, x_bank, gate_w[0][1])
                    if j in (5, 6):
                        free_x_after_wo(g, 2 * (j - 5) + 1)
                        project_out(g, 0, 2 * (j - 5) + 1, x_bank[:, :])
                    if j == 7 and not last:
                        turn_v(g, 2)
                    if last and j == 6:
                        turn_f(1)
                    if last and j == 7:
                        free_x_after_wo(g, TT)
                        turn_f(3)

            def turn_x(b, chunks):
                for k in chunks:
                    if b == 1:
                        pe.wait_ge(h_ready[1 if k >= 2 else 0], k - 1 if k >= 2 else KC)
                    for i in range(TT):
                        last = pe.transpose(ln_banks[b][k][:, i * P:(i + 1) * P],
                                            acc[:, TT * b + i, k * P:(k + 1) * P], ident[:, :])
                    last.then_inc(x_turned, 1)

            def warm(count):
                for _ in range(count):
                    pe.matmul(x_bank[:, :], zeros[:, 0:P], zeros, start=True, stop=True)

            pe.wait_ge(zeros_made, 1)
            warm(6)
            pe.wait_ge(c_ready, 1)
            def modulation_rows(m):
                pe.wait_ge(wmod_in[m], 16)
                for k in range(KC):
                    last = pe.matmul(mod_banks[m][0:B, :], c_silu[:, :, k], wmod_blocks[m][:, k, :],
                                     start=(k == 0), stop=(k == KC - 1))
                last.then_inc(mod_rows, 1)

            def turn_rows(m):
                pe.wait_ge(mod_rows_copied, m + 1)
                for n in range(KC):
                    at = 2 * (KC * m + n)
                    last = pe.transpose(o_bank[:, at:at + 2], mod_row[m][:, n * P:(n + 1) * P], ident[0:B, 0:B])
                last.then_inc(mod_made, 1)

            modulation_rows(0)
            pe.wait_ge(ident_in, 16)
            pe.wait_ge(x_normed, TT)
            turn_x(0, range(KC))
            modulation_rows(1)
            turn_rows(0)
            warm(1)
            turn_rows(1)
            warm(3)
            project_k(0, 0, 0, h_lo[0])
            project_q(0, 0)
            pe.wait_ge(k_copied, 1)
            project_v(0, 0, 0)
            project_q(0, 1)
            turn_v(0, 0)
            pe.wait_ge(x_normed, B * TT)
            turn_x(1, (0, 1))

            group(0, first=True)
            with pe.Fori(1, KV - 1) as g:
                group(g)
            group(KV - 1, last=True)

            turn_probs(KV - 1, STEPS - 1, final=True)
            turn_f(4)
            turn_f(5)
            attend(KV - 1, STEPS - 1)
            for b in range(B):
                turn_gate(B + b, ln2_banks[0][b], gate_w[1][b])

            def turn_x1(b):
                pe.wait_ge(x1_normed, TT * (b + 1))
                for k in range(KC):
                    for i in range(TT):
                        last = pe.transpose(ln2_banks[b][k][:, i * P:(i + 1) * P], xn2[:, i, k * P:(k + 1) * P], ident[:, :])
                    last.then_inc(h2_turned, 1)

            turn_f(6)
            turn_f(7)
            for i in range(TT):
                project_out(KV - 1, 1, i, out_banks[i][:, :])
                if i < 2:
                    turn_f(2 * KC + 2 * i)
                    turn_f(2 * KC + 2 * i + 1)
                if i == 2:
                    pe.wait_ge(f_lo, 3 * KC)
                    pe.wait_ge(gate_copied, 2 * B)
                    turn_x1(0)

            def up(b, m):
                u = TT * b + m
                if u >= 2:
                    pe.wait_ge(x4_made, u - 1)
                for half in range(2):
                    col = half * FF + m * P
                    todo = [(k, a, bb) for k in range(KC) for a, bb in PARTS]
                    for n, (k, a, bb) in enumerate(todo):
                        if m == 0 and half == 0 and (a, bb) == PARTS[0]:
                            pe.wait_ge(h2_lo[b], k + 1)
                        last = pe.matmul(up_banks[u % 2][half][:, :], w12T[a][:, k, col:col + P],
                                         h2T[bb][:, REP * b + k, :], start=(n == 0), stop=(n == len(todo) - 1))
                    last.then_inc(up_made, 1)

            def down(b):
                for ms in ([0, 1], [2], [3]):
                    pe.wait_ge(x4_lo, KC * b + ms[-1] + 1)
                    for i in range(TT):
                        for m in ms:
                            for a, bb in PARTS:
                                last = pe.matmul(out_banks[i][:, :], x4_at(a, b, m)[:, i * P:(i + 1) * P], w3T[bb][:, m, :],
                                                 start=(m == 0 and (a, bb) == PARTS[0]),
                                                 stop=(m == FF // P - 1 and (a, bb) == PARTS[-1]))
                        if ms[-1] == FF // P - 1:
                            last.then_inc(down_made, 1)

            for m in range(FF // P):
                up(0, m)
                if m == 2:
                    pe.wait_ge(wo_added, STEPS * KV)
                    turn_x1(1)
            up(1, 0)
            pe.wait_ge(h2_ready, B * KC)
            down(0)
            for m in range(1, FF // P):
                up(1, m)
            pe.wait_ge(y_made, TT)
            down(1)

        @block.vector
        def _(dve):
            chain = [0]

            def link(ins):
                chain[0] += 1
                ins.then_inc(dve_chain, 1)
                dve.wait_ge(dve_chain, chain[0])

            def cosine_k(g, m_off):
                need(dve, k_copied, 2, g, m_off + 1)
                nc.vector.tensor_tensor(k_tmp[:, 0, :], k_tmp[:, 0, :], cos_sb[:, :], ALU.mult).then_inc(k_cos, 1)

            def cosine_q(g, j):
                need(dve, q_copied, STEPS, g, j + 1)
                part = q_tmp[:, j % 2, 0, :]
                nc.vector.tensor_tensor(part, part, cos_sb[:, :], ALU.mult).then_inc(q_cos, 1)

            def maxima(g, j):
                s = j % 2
                need(dve, pT_turned, 3 * STEPS, g, 3 * (j - 1))
                for k, tiles in enumerate(((1,), (2, 0), (3,))):
                    need(dve, scores_ready, 3 * STEPS, g, 3 * j + k + 1)
                    nc.vector.memset(wait_mark[:, s, k:k + 1], 0.0)
                    for i in tiles:
                        last = nc.vector.tensor_tensor_reduce(
                            probs[:, s, ROW_AT[i]:ROW_AT[i] + ROW_W[i]], s_out[i], mask_sb[:, T - ROW_W[i]:T],
                            1.0, LOWEST, ALU.add, ALU.max, row_max[:, s, i:i + 1])
                    last.then_inc(rows_maxed, 1)
                need(dve, rows_maxed, 3 * STEPS, g, 3 * j + 3)
                nc.vector.tensor_scalar(neg_max[:, s, :], row_max[:, s, :], -SCALE, None, ALU.mult).then_inc(negmax_ready, 1)

            def normalise(g, j):
                s = j % 2
                need(dve, exp_done, STEPS, g, j + 1)
                nc.vector.reciprocal(row_inv[:, s, :], row_sum[:, s, :]).then_inc(inv_ready, 1)
                need(dve, inv_ready, STEPS, g, j + 1)
                for i in range(TT):
                    span = probs[:, s, ROW_AT[i]:ROW_AT[i] + ROW_W[i]]
                    last = nc.vector.tensor_scalar(span, span, row_inv[:, s, i:i + 1], None, ALU.mult)
                last.then_inc(probs_normed, 1)

            def probs_low(g, j):
                for k, (lo, hi) in enumerate(T_BANKS):
                    need(dve, pT_hi, 3 * STEPS, g, 3 * j + k + 1)
                    nc.vector.tensor_tensor(pT[1][:, lo:hi], t_banks[k], pT[0][:, lo:hi].bitcast(f32),
                                            ALU.subtract).then_inc(pT_lo, 1)

            def attn_low(g, j):
                need(dve, attn_hi, STEPS, g, j + 1)
                s = j % STEPS
                nc.vector.tensor_tensor(attn[1][:, s, :], o_bank[:, :], attn[0][:, s, :].bitcast(f32),
                                        ALU.subtract).then_inc(attn_lo, 1)

            def v_low(g, b, m_off):
                need(dve, v_hi, 2, g, m_off + 1)
                nc.vector.tensor_tensor(v_flat[1][:, b, :], x_bank[:, :], v_flat[0][:, b, :].bitcast(f32),
                                        ALU.subtract).then_inc(v_lo, 1)

            def add_out(g, w, w_off, first=False, src=None):
                src = x_bank if src is None else src
                need(dve, wo_made, STEPS, g, w_off + 1)
                if first:
                    nc.vector.tensor_copy(acc[:, w, :], src[:, :]).then_inc(wo_added, 1)
                else:
                    nc.vector.tensor_tensor(acc[:, w, :], src[:, :], acc[:, w, :], ALU.add).then_inc(wo_added, 1)

            def group(g, first=False, last=False):
                for j in range(STEPS):
                    maxima(g, j)
                    if first and j == 0:
                        h_low(2)
                        h_low(3)
                    if first and j == 1:
                        cosine_k(g, 1)
                    if not (first and j == 0):
                        probs_low(g, j - 1)
                    if first and j == 1:
                        dve.wait_ge(mod_made, 4)
                        nc.vector.tensor_copy(mod[:, 2 * KC:3 * KC, :].rearrange("p m b -> p (m b)"),
                                              o_bank[:, 4 * KC:6 * KC]).then_inc(mod_read, 1)
                    normalise(g, j)
                    if last and j == 7:
                        f_low(2)
                    if not (last and j + 2 >= STEPS):
                        cosine_q(g, j + 2)
                    if j in (1, 2) and not first:
                        add_out(g, TT + 2 * (j - 1), -TT + 2 * (j - 1))
                    if j in (5, 6):
                        add_out(g, 2 * (j - 5), 2 * (j - 5), first=first)
                    if last and j == 6:
                        f_low(0)
                    if j == 0 and not first:
                        cosine_k(g, 1)
                    if j == 4 and not last:
                        cosine_k(g, 2)
                    if not (first and j == 0):
                        attn_low(g, j - 1)
                    if first and j == 2:
                        dve.wait_ge(mod_made, 10)
                        nc.vector.tensor_copy(mod[:, 3 * KC:6 * KC, :].rearrange("p m b -> p (m b)"),
                                              x_bank[:, 6 * KC:12 * KC]).then_inc(mod_read, 1)
                        dve.wait_ge(mod_read, 2)
                        nc.vector.memset(acc[:, TT:2 * TT, :], 0.0)
                        nc.vector.tensor_scalar(one_plus[:, KC:2 * KC, :], mod[:, 4 * KC:5 * KC, :], 1.0, None, ALU.add)
                        for a, m in enumerate((2, 5)):
                            src = mod[:, m * KC:(m + 1) * KC, :]
                            sign = gate_sign[:, a * KC:(a + 1) * KC, :]
                            size = gate[:, a * KC:(a + 1) * KC, :]
                            link(nc.vector.tensor_scalar(sign, src, 0.0, 2.0, ALU.is_ge, ALU.mult))
                            link(nc.vector.tensor_scalar(sign, sign, -1.0, None, ALU.add))
                            link(nc.vector.tensor_tensor(size, src, sign, ALU.mult))
                            link(nc.vector.tensor_scalar(size, size, 0.25, None, ALU.max))
                            link(nc.vector.tensor_tensor(size, size, sign, ALU.mult))
                    if j in (1, 2) and not first:
                        add_out(g, TT + 2 * (j - 1) + 1, -TT + 2 * (j - 1) + 1)
                    if j in (5, 6):
                        add_out(g, 2 * (j - 5) + 1, 2 * (j - 5) + 1, first=first)
                    if j == 3:
                        v_low(g, 1, 1)
                    if j == 7 and not last:
                        v_low(g, 0, 2)
                    if last and j == 3:
                        dve.wait_ge(k_lo, 2 * KV)
                        for b in range(B):
                            spread_gate(0, b)
                    if last and j == 6:
                        f_low(1)
                    if last and j == 7:
                        dve.wait_ge(q_sum, STEPS * KV)
                        for b in range(B):
                            spread_gate(1, b)
                        f_low(3)
                        x1_stats(0)

            def moments_of(b, done):
                dve.wait_ge(stats_made, TT * done)
                for w in range(TT * b, TT * (b + 1)):
                    last = nc.vector.bn_aggr(moments[:, w, :], stats[:, w, :])
                last.then_inc(moments_ready, 1)
                dve.wait_ge(moments_ready, done)

            def norm_scale(b, done):
                moments_of(b, done)
                w = slice(TT * b, TT * (b + 1))
                v, y, t = var_eps[:, w, :], rstd[:, w, :], newton[:, w, :]
                link(nc.vector.tensor_scalar(v, moments[:, w, 1:2], EPS, None, ALU.add))
                link(nc.vector.tensor_scalar(y.bitcast(i32), v.bitcast(i32), -0.5, float(0x5f3759df), ALU.mult, ALU.add))
                for _ in range(3):
                    link(nc.vector.tensor_tensor(t, y, y, ALU.mult))
                    link(nc.vector.scalar_tensor_tensor(out=t, in0=t, scalar=-0.5, in1=v, op0=ALU.mult, op1=ALU.mult))
                    link(nc.vector.scalar_tensor_tensor(out=y, in0=t, scalar=1.5, in1=y, op0=ALU.add, op1=ALU.mult))
                nc.vector.scalar_tensor_tensor(out=shift[:, w, :], in0=moments[:, w, 0:1], scalar=-1.0, in1=y,
                                               op0=ALU.mult, op1=ALU.mult).then_inc(norm_ready, 1)

            def f_low(u):
                dve.wait_ge(f_hi, u + 1)
                dst = f_place(u)
                nc.vector.tensor_tensor(dst[1], f_banks[u][:, :], dst[0].bitcast(f32), ALU.subtract).then_inc(f_lo, 1)

            def spread_gate(a, b):
                nc.vector.tensor_copy(gate_w[a][b].rearrange("p (k t) -> p k t", k=KC),
                                      gate[:, a * KC:(a + 1) * KC, b:b + 1].to_broadcast([P, KC, P])).then_inc(gate_wide, 1)

            def x1_stats(w):
                dve.wait_ge(x1_made, w + 1)
                nc.vector.bn_stats(stats[:, w, :], acc[:, w, :]).then_inc(stats_made, 1)

            nc.vector.memset(zeros, 0.0).then_inc(zeros_made, 1)
            dve.wait_ge(c_exped, 1)
            link(nc.vector.tensor_scalar(c_exp[:, :, :], c_exp[:, :, :], 1.0, None, ALU.add))
            link(nc.vector.reciprocal(c_silu[:, :, :], c_exp[:, :, :]))
            nc.vector.tensor_tensor(c_silu[:, :, :], c_silu[:, :, :], cT[:, :, :], ALU.mult).then_inc(c_ready, 1)

            def norm_x(b):
                for w in range(TT * b, TT * (b + 1)):
                    nc.vector.tensor_scalar(acc[:, w, :], acc[:, w, :], moments[:, w, 0:1], rstd[:, w, :],
                                            ALU.subtract, ALU.mult).then_inc(x_normed, 1)

            for w in range(TT):
                if w % 2 == 0:
                    dve.wait_ge(x_in[w // 2], 16)
                nc.vector.bn_stats(stats[:, w, :], acc[:, w, :]).then_inc(stats_made, 1)
            norm_scale(0, 1)
            norm_x(0)
            dve.wait_ge(mod_made, 2)
            link(nc.vector.tensor_copy(mod[:, 0:2 * KC, :].rearrange("p m b -> p (m b)"), o_bank[:, 0:4 * KC]))
            nc.vector.tensor_scalar(one_plus[:, 0:KC, :], mod[:, KC:2 * KC, :], 1.0, None, ALU.add).then_inc(mod_ready, 1)
            for k in range(KC):
                dve.wait_ge(h_ready[0], k + 1)
                nc.vector.tensor_copy(hT[0][:, k, 0:T], h_tmp[0][k]).then_inc(h_hi[0], 1)
                dve.wait_ge(h_hi[0], k + 1)
                nc.vector.tensor_tensor(hT[1][:, k, 0:T], h_tmp[0][k], hT[0][:, k, 0:T].bitcast(f32),
                                        ALU.subtract).then_inc(h_lo[0], 1)
            def low_part(parts, at, src, hi, count, done):
                dve.wait_ge(hi, count)
                nc.vector.tensor_tensor(parts[1][at], src, parts[0][at].bitcast(f32), ALU.subtract).then_inc(done, 1)

            def h_low(k):
                low_part(hT, (slice(None), k, slice(T, 2 * T)), h_tmp[1][k], h_hi[1], k + 1, h_lo[1])

            dve.wait_ge(tables_in, 48)
            dve.wait_ge(x_in[2], 16)
            for w in range(TT, 2 * TT):
                nc.vector.bn_stats(stats[:, w, :], acc[:, w, :]).then_inc(stats_made, 1)
            cosine_k(0, 0)
            norm_scale(1, 2)
            cosine_q(0, 0)
            low_part(kT, (slice(None), 0), k_tmp[:, 0, :], k_hi, 1, k_lo)
            norm_x(1)
            low_part(qT, (slice(None), 0), q_tmp[:, 0, 0, :], q_hi, 1, q_lo)
            cosine_q(0, 1)
            h_low(0)
            v_low(0, 0, 0)
            h_low(1)

            group(0, first=True)
            with dve.Fori(1, KV - 1) as g:
                group(g)
            group(KV - 1, last=True)

            probs_low(KV - 1, STEPS - 1)
            f_low(4)
            f_low(5)
            attn_low(KV - 1, STEPS - 1)
            f_low(6)
            f_low(7)
            for w in range(1, TT):
                x1_stats(w)
            norm_scale(0, B + 1)

            def h2_low(k):
                low_part(h2T, (slice(None), k), h2_tmp[k], h2_hi[0], k + 1, h2_lo[0])

            add_out(KV - 1, TT, TT, src=out_banks[0])
            f_low(2 * KC)
            f_low(2 * KC + 1)
            add_out(KV - 1, TT + 1, TT + 1, src=out_banks[1])
            f_low(2 * KC + 2)
            f_low(2 * KC + 3)
            x1_stats(TT)
            h2_low(0)
            h2_low(1)
            add_out(KV - 1, TT + 2, TT + 2, src=out_banks[2])
            h2_low(2)
            h2_low(3)
            x1_stats(TT + 1)
            add_out(KV - 1, TT + 3, TT + 3, src=out_banks[3])
            x1_stats(TT + 2)

            def gate_up(u):
                m = u % TT
                e, r = up_tmp[u % 2]
                x1b, x2b = up_banks[u % 2]
                dve.wait_ge(e_made, u + 1)
                link(nc.vector.tensor_scalar(e, e, 1.0, None, ALU.add))
                link(nc.vector.reciprocal(r, e))
                link(nc.vector.scalar_tensor_tensor(out=e, in0=x1b[:, :], scalar=b12T[:, m:m + 1], in1=r,
                                                    op0=ALU.add, op1=ALU.mult))
                dve.wait_ge(up_made, 2 * (u + 1))
                nc.vector.scalar_tensor_tensor(out=r, in0=x2b[:, :], scalar=b12T[:, KC + m:KC + m + 1], in1=e,
                                               op0=ALU.add, op1=ALU.mult).then_inc(x4_made, 1)

            def finish(b):
                if b == 1:
                    dve.wait_ge(y_made, TT)
                for i in range(TT + 1):
                    if i < TT:
                        dve.wait_ge(down_made, TT * b + i + 1)
                        nc.vector.tensor_tensor(y_tmp[i], out_banks[i][:, :], gate_w[1][b], ALU.mult).then_inc(down_gated, 1)
                    if i >= 1:
                        w = TT * b + i - 1
                        dve.wait_ge(down_gated, w + 1)
                        dve.wait_ge(x1_b3, w + 1)
                        nc.vector.tensor_tensor(acc[:, w, :], acc[:, w, :], y_tmp[i - 1], ALU.add).then_inc(y_made, 1)

            gate_up(0)
            x1_stats(2 * TT - 1)
            norm_scale(1, B + 2)
            for u in range(1, TT + 1):
                gate_up(u)
            finish(0)
            for u in range(TT + 1, 2 * TT):
                gate_up(u)
            finish(1)

        @block.scalar
        def _(act):
            def split_hi(dst, src, done):
                nc.scalar.activation(dst, src, ACT.Copy).then_inc(done, 1)

            def wq_high(g, h, g_off):
                need(act, wq_in, 16, g, 16 * (g_off + 1))
                need(act, q_proj, STEPS, g, STEPS * g_off - REP + h + 1)
                split_hi(wq_s[0][:, h, :, :], wq_raw[:, :, h * HD:(h + 1) * HD], wq_hi)

            def wk_high(g, g_off):
                need(act, wk_in, 16, g, 16 * (g_off + 1))
                need(act, k_proj, 2, g, 2 * g_off)
                split_hi(wk_s[0][:, :, :], wk_raw[:, :, :], wk_hi)

            def wv_high(g, g_off):
                need(act, wv_in, 16, g, 16 * (g_off + 1))
                need(act, v_proj, 2, g, 2 * g_off)
                split_hi(wv_s[0][:, :, :], wv_raw[:, :, :], wv_hi)

            def wo_high(g, r, first):
                need(act, wo_in, 16, g, 16)
                need(act, wo_made, STEPS, g, 0)
                if first:
                    act.wait_ge(mod_made, 10)
                split_hi(wo_s[0][:, r, :], wo_raw[:, r, :], wo_hi)

            def probs_high(g, j):
                need(act, attn_done, STEPS, g, j)
                for k, (lo, hi) in enumerate(T_BANKS):
                    need(act, pT_turned, 3 * STEPS, g, 3 * j + k + 1)
                    split_hi(pT[0][:, lo:hi], t_banks[k], pT_hi)

            def exponents(g, j):
                s = j % 2
                need(act, negmax_ready, STEPS, g, j + 1)
                for i in range(TT):
                    span = probs[:, s, ROW_AT[i]:ROW_AT[i] + ROW_W[i]]
                    last = nc.scalar.activation(span, span, ACT.Exp, bias=neg_max[:, s, i:i + 1], scale=SCALE,
                                                accum_out=row_sum[:, s, i:i + 1])
                last.then_inc(exp_done, 1)

            half = HD // 2

            def copy_turned(src, plain, swapped):
                nc.scalar.activation(plain, src[:, :], ACT.Copy)
                nc.scalar.activation(swapped[0:half, :], src[half:HD, :], ACT.Copy)
                return nc.scalar.activation(swapped[half:HD, :], src[0:half, :], ACT.Copy)

            def q_copy(g, j):
                need(act, q_lo, STEPS, g, j - 1)
                need(act, q_proj, STEPS, g, j + 1)
                copy_turned(q_bank, q_tmp[:, j % 2, 0, :], q_tmp[:, j % 2, 1, :]).then_inc(q_copied, 1)

            def k_copy(g, m_off):
                need(act, k_lo, 2, g, m_off)
                need(act, k_proj, 2, g, m_off + 1)
                copy_turned(x_bank, k_tmp[:, 0, :], k_tmp[:, 1, :]).then_inc(k_copied, 1)

            def q_high(g, j):
                need(act, scores_ready, 3 * STEPS, g, 3 * (j - 1))
                need(act, q_sum, STEPS, g, j + 1)
                split_hi(qT[0][:, j % 2, :], q_tmp[:, j % 2, 0, :], q_hi)

            def k_high(g, b, m_off):
                need(act, scores_ready, 3 * STEPS, g, 3 * REP * (m_off - 1))
                need(act, k_sum, 2, g, m_off + 1)
                split_hi(kT[0][:, b, :], k_tmp[:, 0, :], k_hi)

            def v_copy(g, m_off):
                need(act, v_turned, 2, g, m_off)
                need(act, v_proj, 2, g, m_off + 1)
                split_hi(vT[:, :], x_bank[:, :], v_copied)

            def v_high(g, b, m_off):
                need(act, attn_done, STEPS, g, REP * (m_off - 1))
                need(act, v_turned, 2, g, m_off + 1)
                split_hi(v_flat[0][:, b, :], x_bank[:, :], v_hi)

            def attn_high(g, j):
                need(act, attn_done, STEPS, g, j + 1)
                if j >= 0:
                    need(act, wo_made, STEPS, g, TT * (j // REP - 1))
                split_hi(attn[0][:, j % STEPS, :], o_bank[:, :], attn_hi)

            def modulate_x(b, k):
                act.wait_ge(x_turned, KC * b + k + 1)
                if b == 1 and k >= 2:
                    act.wait_ge(h_lo[1], k - 1)
                if b == 1 and k == 0:
                    act.wait_ge(k_lo, 1)
                nc.scalar.activation(h_tmp[b][k], ln_banks[b][k][:, :], ACT.Identity, bias=mod[:, k, b:b + 1],
                                     scale=one_plus[:, k, b:b + 1]).then_inc(h_ready[b], 1)
                if b == 1:
                    act.wait_ge(h_ready[1], k + 1)
                    split_hi(hT[0][:, k, T:2 * T], h_tmp[1][k], h_hi[1])

            def f_high(u):
                act.wait_ge(f_turned, u + 1)
                split_hi(f_place(u)[0], f_banks[u][:, :], f_hi)

            def gate_copy(n, bank):
                act.wait_ge(gate_turned, n + 1)
                split_hi(gate_w[n // B][n % B], bank[:, :], gate_copied)

            def group(g, first=False, last=False):
                for j in range(STEPS):
                    if not (first and j == 0):
                        probs_high(g, j - 1)
                    if first and j == 0:
                        modulate_x(1, 2)
                        modulate_x(1, 3)
                    exponents(g, j)
                    if not (last and j + 2 >= STEPS):
                        q_copy(g, j + 2)
                    if j == 1:
                        k_high(g, 1, 1)
                    if j == 5 and not last:
                        k_high(g, 0, 2)
                    if last and j == 4:
                        gate_copy(0, x_bank)
                    if last and j >= 6:
                        f_high((0, 2)[j - 6])
                    if j == 0:
                        k_copy(g, 1)
                    if j == 4 and not last:
                        k_copy(g, 2)
                    if j == 3:
                        v_copy(g, 1)
                    if j == 7 and not last:
                        v_copy(g, 2)
                    if not (first and j == 0):
                        attn_high(g, j - 1)
                    if last and j == 4:
                        gate_copy(1, x_bank)
                    if not (last and j + 2 >= STEPS):
                        q_high(g, j + 2)
                    if last and j >= 6:
                        f_high((1, 3)[j - 6])
                    if j == 3:
                        v_high(g, 1, 1)
                    if j == 7 and not last:
                        v_high(g, 0, 2)
                    if j == 1 and not last:
                        wk_high(g, 1)
                    if j == 5 and not last:
                        wv_high(g, 1)
                    if j >= 4 and not last:
                        wq_high(g, j - 4, 1)
                    if j == 3:
                        for r in range(REP):
                            wo_high(g, r, first)

            act.dma_start(cT[:, :, :], c.rearrange("b (p k) -> p b k", p=P)).then_inc(c_in, 16)
            act.dma_start(ident[:, :], ident_t).then_inc(ident_in, 16)
            act.wait_ge(c_in, 16)
            nc.scalar.activation(c_exp[:, :, :], cT[:, :, :], ACT.Exp, scale=-1.0).then_inc(c_exped, 1)
            wk_high(0, 0)
            act.wait_ge(wq0_in, 16)
            split_hi(wq_s[0][:, 0, :, :], wq_raw[:, :, 0:HD], wq_hi)
            for m in range(2):
                act.wait_ge(mod_rows, m + 1)
                split_hi(mod_row[m], mod_banks[m][0:B, :], mod_rows_copied)
            act.wait_ge(mod_ready, 1)
            for k in range(KC):
                modulate_x(0, k)
            wv_high(0, 0)
            wq_high(0, 1, 0)
            k_copy(0, 0)
            q_copy(0, 0)
            k_high(0, 0, 0)
            wq_high(0, 2, 0)
            q_high(0, 0)
            v_copy(0, 0)
            wq_high(0, 3, 0)
            q_copy(0, 1)
            modulate_x(1, 0)
            v_high(0, 0, 0)
            modulate_x(1, 1)
            q_high(0, 1)

            group(0, first=True)
            act.wait_ge(b_in, 16)
            nc.scalar.activation(neg_b1[:, :], b12T[:, 0:KC], ACT.Copy, scale=-1.0)
            with act.Fori(1, KV - 1) as g:
                group(g)
            group(KV - 1, last=True)

            probs_high(KV - 1, STEPS - 1)
            f_high(4)
            f_high(5)
            attn_high(KV - 1, STEPS - 1)
            for b in range(B):
                gate_copy(B + b, ln2_banks[0][b])
            for u in range(6, 2 * KC + 2):
                f_high(u)

            def norm_x1(b):
                act.wait_ge(norm_ready, B + b + 1)
                if b == 1:
                    act.wait_ge(h2_turned, KC)
                for w in range(TT * b, TT * (b + 1)):
                    nc.scalar.activation(xn2[:, w % TT, :], acc[:, w, :], ACT.Identity, bias=shift[:, w, :],
                                         scale=rstd[:, w, :]).then_inc(x1_normed, 1)

            def modulate_x1(b):
                if b == 1:
                    act.wait_ge(h2_lo[0], KC)
                for k in range(KC + 1):
                    if k < KC:
                        act.wait_ge(h2_turned, KC * b + k + 1)
                        nc.scalar.activation(h2_tmp[k], ln2_banks[b][k][:, :], ACT.Identity,
                                             bias=mod[:, 3 * KC + k, b:b + 1],
                                             scale=one_plus[:, KC + k, b:b + 1]).then_inc(h2_ready, 1)
                    if k >= 1:
                        act.wait_ge(h2_ready, KC * b + k)
                        split_hi(h2T[0][:, REP * b + k - 1, :], h2_tmp[k - 1], h2_hi[b])

            def up_exp(u):
                act.wait_ge(up_made, 2 * u + 1)
                if u >= 2:
                    act.wait_ge(x4_lo, u - 1)
                nc.scalar.activation(up_tmp[u % 2][0], up_banks[u % 2][0][:, :], ACT.Exp,
                                     bias=neg_b1[:, u % TT:u % TT + 1], scale=-1.0).then_inc(e_made, 1)

            norm_x1(0)
            f_high(2 * KC + 2)
            f_high(2 * KC + 3)
            modulate_x1(0)
            up_exp(0)
            for u in range(B * TT):
                if u + 1 < B * TT:
                    up_exp(u + 1)
                if u == 1:
                    modulate_x1(1)
                act.wait_ge(x4_made, u + 1)
                split_hi(x4_at(0, u // TT, u % TT), up_tmp[u % 2][1], x4_hi)
                if u == 0:
                    norm_x1(1)

        @block.gpsimd
        def _(pool):
            def split_lo(dst, src, hi, done):
                nc.gpsimd.tensor_tensor(dst, src, hi.bitcast(f32), ALU.subtract).then_inc(done, 1)

            def wq_low(g, h, g_off):
                need(pool, wq_hi, REP, g, REP * g_off + h + 1)
                split_lo(wq_s[1][:, h, :, :], wq_raw[:, :, h * HD:(h + 1) * HD], wq_s[0][:, h, :, :], wq_lo)

            def wk_low(g, g_off):
                need(pool, wk_hi, 1, g, g_off + 1)
                split_lo(wk_s[1][:, :, :], wk_raw[:, :, :], wk_s[0][:, :, :], wk_lo)

            def wv_low(g, g_off):
                need(pool, wv_hi, 1, g, g_off + 1)
                split_lo(wv_s[1][:, :, :], wv_raw[:, :, :], wv_s[0][:, :, :], wv_lo)

            def wo_low(g, r):
                need(pool, wo_hi, REP, g, r + 1)
                split_lo(wo_s[1][:, r, :], wo_raw[:, r, :], wo_s[0][:, r, :], wo_lo)

            def q_turn(g, j):
                a, b = q_tmp[:, j % 2, 0, :], q_tmp[:, j % 2, 1, :]
                need(pool, q_copied, STEPS, g, j + 1)
                nc.gpsimd.tensor_tensor(b, b, sin_sb[:, :], ALU.mult).then_inc(q_sin, 1)
                need(pool, q_sin, STEPS, g, j + 1)
                need(pool, q_cos, STEPS, g, j + 1)
                nc.gpsimd.tensor_tensor(a, a, b, ALU.add).then_inc(q_sum, 1)

            def q_low(g, j):
                need(pool, q_hi, STEPS, g, j + 1)
                split_lo(qT[1][:, j % 2, :], q_tmp[:, j % 2, 0, :], qT[0][:, j % 2, :], q_lo)

            def k_turn(g, m_off):
                a, b = k_tmp[:, 0, :], k_tmp[:, 1, :]
                need(pool, k_copied, 2, g, m_off + 1)
                nc.gpsimd.tensor_tensor(b, b, sin_sb[:, :], ALU.mult).then_inc(k_sin, 1)
                need(pool, k_sin, 2, g, m_off + 1)
                need(pool, k_cos, 2, g, m_off + 1)
                nc.gpsimd.tensor_tensor(a, a, b, ALU.add).then_inc(k_sum, 1)

            def k_low(g, b, m_off):
                need(pool, k_hi, 2, g, m_off + 1)
                split_lo(kT[1][:, b, :], k_tmp[:, 0, :], kT[0][:, b, :], k_lo)

            def group(g, first=False, last=False):
                for j in range(STEPS):
                    if not (last and j + 2 >= STEPS):
                        q_turn(g, j + 2)
                    if j == 1:
                        k_low(g, 1, 1)
                    if j == 5 and not last:
                        k_low(g, 0, 2)
                    if j == 0:
                        k_turn(g, 1)
                    if j == 4 and not last:
                        k_turn(g, 2)
                    if not (last and j + 2 >= STEPS):
                        q_low(g, j + 2)
                    if last and j >= 6:
                        first_residual(2 * (j - 6))
                        first_residual(2 * (j - 6) + 1)
                    if j == 1 and not last:
                        wk_low(g, 1)
                    if j == 5 and not last:
                        wv_low(g, 1)
                    if j >= 4 and not last:
                        wq_low(g, j - 4, 1)
                    if j == 3:
                        for r in range(REP):
                            wo_low(g, r)

            def first_residual(w):
                pool.wait_ge(wo_added, STEPS * (KV - 1) + w + 1)
                pool.wait_ge(gate_copied, w // TT + 1)
                nc.gpsimd.tensor_tensor(acc[:, w, :], acc[:, w, :], gate_w[0][w // TT], ALU.mult).then_inc(x_gated, 1)
                pool.wait_ge(x_gated, w + 1)
                pool.wait_ge(xr_in[w % 2], 16 * (w // 2 + 1))
                nc.gpsimd.tensor_tensor(acc[:, w, :], acc[:, w, :], x_ring[w % 2], ALU.add).then_inc(x1_made, 1)

            wk_low(0, 0)
            wq_low(0, 0, 0)
            wv_low(0, 0)
            wq_low(0, 1, 0)
            pool.wait_ge(tables_in, 48)
            k_turn(0, 0)
            q_turn(0, 0)
            wq_low(0, 2, 0)
            q_turn(0, 1)
            wq_low(0, 3, 0)
            q_low(0, 1)

            group(0, first=True)
            with pool.Fori(1, KV - 1) as g:
                group(g)
            group(KV - 1, last=True)

            def h2_low(k):
                pool.wait_ge(h2_hi[1], k + 1)
                split_lo(h2T[1][:, REP + k, :], h2_tmp[k], h2T[0][:, REP + k, :], h2_lo[1])

            def x4_low(u):
                pool.wait_ge(x4_hi, u + 1)
                split_lo(x4_at(1, u // TT, u % TT), up_tmp[u % 2][1], x4_at(0, u // TT, u % TT), x4_lo)

            def gate_bias(b):
                if b == 0:
                    pool.wait_ge(rows_maxed, 3 * STEPS * KV)
                    pool.wait_ge(gate_copied, 2 * B)
                    pool.wait_ge(b3_in, 16)
                else:
                    pool.wait_ge(gate_b3, 1)
                nc.gpsimd.tensor_tensor(gate_b3_w[b], b3_w, gate_w[1][b], ALU.mult).then_inc(gate_b3, 1)

            def add_bias(w):
                pool.wait_ge(x1_normed, w + 1)
                pool.wait_ge(gate_b3, w // TT + 1)
                nc.gpsimd.tensor_tensor(acc[:, w, :], acc[:, w, :], gate_b3_w[w // TT], ALU.add).then_inc(x1_b3, 1)

            for w in range(TT, 2 * TT):
                first_residual(w)
            gate_bias(0)
            x4_low(0)
            add_bias(0)
            add_bias(1)
            for k in range(KC):
                h2_low(k)
            x4_low(1)
            add_bias(2)
            add_bias(3)
            x4_low(2)
            gate_bias(1)
            x4_low(3)
            for i in range(TT):
                add_bias(TT + i)
            for u in range(TT, 2 * TT):
                x4_low(u)


def rope_tables():
    theta, factor, hi_ff, lo_ff, orig_max = 500000.0, 8.0, 4.0, 1.0, 1024
    inv = 1.0 / theta ** (np.arange(0, HD, 2, dtype=np.float64) / HD)
    wavelen = 2.0 * np.pi / inv
    smooth = (orig_max / wavelen - lo_ff) / (hi_ff - lo_ff)
    scaled = np.where(wavelen > orig_max / lo_ff, inv / factor, inv)
    mid = (wavelen <= orig_max / lo_ff) & (wavelen >= orig_max / hi_ff)
    scaled = np.where(mid, (1 - smooth) * inv / factor + smooth * inv, scaled).astype(np.float32)
    freqs = np.arange(T, dtype=np.float32)[:, None] * scaled[None, :]
    cos, sin = np.cos(freqs).T, np.sin(freqs).T
    return (np.ascontiguousarray(np.concatenate([cos, cos])).astype(np.float32),
            np.ascontiguousarray(np.concatenate([-sin, sin])).astype(np.float32))


def causal_mask():
    mask = np.zeros((P, T), np.float32)
    mask[:, T - P:][np.triu_indices(P, 1)] = MASKED
    return mask


_INS = ['L0_attn_x', 'L0_attn_wq', 'L0_attn_wk', 'L0_attn_wv', 'L0_attn_wo', 'L0_ffn_w12', 'L0_ffn_b12',
        'L0_ffn_w3', 'L0_ffn_b3', 'L0_c', 'L0_wmod']


def kernel(**inputs):
    import concourse.bacc as _bacc
    from concourse.bass_utils import run_bass_kernel_spmd as _run

    nc = _bacc.Bacc("TRN2", target_bir_lowering=False, num_devices=1)
    cos, sin = rope_tables()
    given = [(n, np.ascontiguousarray(inputs[n])) for n in _INS]
    given += [("rope_cos", cos), ("rope_sin", sin), ("causal_mask", causal_mask()),
              ("identity", np.eye(P, dtype=np.float32))]
    arrays, args = {}, []
    for name, a in given:
        arrays[f"in_{name}_dram"] = a
        args.append(nc.dram_tensor(f"in_{name}_dram", a.shape, mybir.dt.from_np(a.dtype), kind="ExternalInput").ap())
    args.append(nc.dram_tensor("out_dram", (B, T, HID), mybir.dt.float32, kind="ExternalOutput").ap())
    adaln_block(nc, *args)
    r = _run(nc, [arrays], core_ids=[0])
    return r.results[0]["out_dram"]
```
